# Optimizing a Trainium2 kernel written in Bass

```python
import numpy as np
import jax
import jax.numpy as jnp

def _softmax(x, axis=-1):
    return jax.nn.softmax(x, axis=axis)

def _gelu(x):
    return jax.nn.gelu(x, approximate=True)

def _silu(x):
    return jax.nn.silu(x)

def _sigmoid(x):
    return jax.nn.sigmoid(x)

def _layernorm(x, axis=-1, eps=1e-05):
    m = jnp.mean(x, axis=axis, keepdims=True)
    v = jnp.var(x, axis=axis, keepdims=True)
    return (x - m) / jnp.sqrt(v + eps)

def _scatter_add(tgt, idx, src, axis=0):
    return tgt.at[idx].add(src)

def _segment_sum(src, seg, n):
    return jax.ops.segment_sum(src, seg, n)
kernel_name = 'mk_gnn_ffn_d1_gnn_r32_04b61f'

def setup_inputs(seed: int=0):
    np.random.seed(seed)
    _w = jnp.asarray

    def _rec_inputs():
        import jax
        import jax.numpy as jnp
        _gk = jax.random.key(seed)
        x = -0.0002117 + 1 * jax.random.normal(jax.random.fold_in(_gk, 1), (10000, 512), jnp.float32)
        _s = jax.random.randint(jax.random.fold_in(_gk, 2), (5000,), 0, 10000, jnp.int32)
        _d = jax.random.randint(jax.random.fold_in(_gk, 3), (5000,), 0, 10000, jnp.int32)
        _loop = jnp.arange(10000, dtype=jnp.int32)
        src = jnp.concatenate([_s, _d, _loop])
        dst = jnp.concatenate([_d, _s, _loop])
        _o = jnp.argsort(dst, stable=True)
        src = src[_o]
        dst = dst[_o]
        return (x, src, dst)
    x, src, dst = _rec_inputs()

    def _L0_gnn_setup():
        import jax, jax.numpy as jnp
        import numpy as np
        BN_EPS = 1e-05
        N_NODES, N_EDGES, D, N_LAYERS = (50000, 12500, 512, 3)
        key = jax.random.key(seed)
        k_x, k_e, k_w = jax.random.split(key, 3)
        x = jax.random.normal(k_x, (N_NODES, D), dtype=jnp.float32)
        edge_index = jax.random.randint(k_e, (2, N_EDGES), 0, N_NODES, dtype=jnp.int64)
        W = jax.random.normal(k_w, (N_LAYERS, D, D), dtype=jnp.float32) * (1.0 / np.sqrt(D))
        b = jnp.zeros((N_LAYERS, D), dtype=jnp.float32)
        gamma = jnp.ones((N_LAYERS, D), dtype=jnp.float32)
        beta = jnp.zeros((N_LAYERS, D), dtype=jnp.float32)
        return {'x': x, 'edge_index': edge_index, 'W': W, 'b': b, 'gamma': gamma, 'beta': beta}
    _L0_gnn_all = _L0_gnn_setup()
    _L0_gnn_in = {k: v for k, v in _L0_gnn_all.items() if k in ('W', 'b', 'gamma', 'beta')}
    del _L0_gnn_all

    def _L0_ffn_setup():
        import jax, jax.numpy as jnp
        import numpy as np
        INPUT_SIZE = 512
        HIDDEN_SIZE = 512
        key = jax.random.key(seed)
        ks = jax.random.split(key, 9)
        B, T, I, H = (64, 512, INPUT_SIZE, HIDDEN_SIZE)
        scale = 1.0 / np.sqrt(I + H)
        x = jax.random.normal(ks[0], (B, T, I), dtype=jnp.float32)

        def lin(kw, kb):
            W = jax.random.uniform(kw, (I + H, H), minval=-scale, maxval=scale, dtype=jnp.float32)
            b = jax.random.uniform(kb, (H,), minval=-scale, maxval=scale, dtype=jnp.float32)
            return (W, b)
        W_f, b_f = lin(ks[1], ks[2])
        W_i, b_i = lin(ks[3], ks[4])
        W_c, b_c = lin(ks[5], ks[6])
        W_o, b_o = lin(ks[7], ks[8])
        return {'x': x, 'W_f': W_f, 'b_f': b_f, 'W_i': W_i, 'b_i': b_i, 'W_c': W_c, 'b_c': b_c, 'W_o': W_o, 'b_o': b_o}
    _L0_ffn_all = _L0_ffn_setup()
    _L0_ffn_in = {k: v for k, v in _L0_ffn_all.items() if k in ('W_f', 'b_f', 'W_i', 'b_i', 'W_c', 'b_c', 'W_o', 'b_o')}
    del _L0_ffn_all
    return {'x': x, 'src': src, 'dst': dst, 'L0_gnn_W': _L0_gnn_in['W'], 'L0_gnn_b': _L0_gnn_in['b'], 'L0_gnn_gamma': _L0_gnn_in['gamma'], 'L0_gnn_beta': _L0_gnn_in['beta'], 'L0_ffn_W_f': _L0_ffn_in['W_f'], 'L0_ffn_b_f': _L0_ffn_in['b_f'], 'L0_ffn_W_i': _L0_ffn_in['W_i'], 'L0_ffn_b_i': _L0_ffn_in['b_i'], 'L0_ffn_W_c': _L0_ffn_in['W_c'], 'L0_ffn_b_c': _L0_ffn_in['b_c'], 'L0_ffn_W_o': _L0_ffn_in['W_o'], 'L0_ffn_b_o': _L0_ffn_in['b_o']}

def reference(x, src, dst, L0_gnn_W, L0_gnn_b, L0_gnn_gamma, L0_gnn_beta, L0_ffn_W_f, L0_ffn_b_f, L0_ffn_W_i, L0_ffn_b_i, L0_ffn_W_c, L0_ffn_b_c, L0_ffn_W_o, L0_ffn_b_o):
    import jax
    import jax.numpy as jnp

    def _L0_gnn_ref(x, W, b, gamma, beta, edge_index):
        import jax, jax.numpy as jnp
        import numpy as np
        BN_EPS = 1e-05
        N_NODES, N_EDGES, D, N_LAYERS = (50000, 12500, 512, 3)
        N = x.shape[0]
        loops = jnp.arange(N, dtype=edge_index.dtype)
        src = jnp.concatenate([edge_index[0], loops])
        dst = jnp.concatenate([edge_index[1], loops])
        deg = jax.ops.segment_sum(jnp.ones(src.shape, jnp.float32), dst, num_segments=N)
        dinv = jax.lax.rsqrt(deg)
        norm = dinv[src] * dinv[dst]
        for l in range(W.shape[0]):
            h = x @ W[l].T
            agg = jax.ops.segment_sum(h[src] * norm[:, None], dst, num_segments=N) + b[l]
            mean = jnp.mean(agg, axis=0)
            var = jnp.mean((agg - mean) ** 2, axis=0)
            xn = (agg - mean) * jax.lax.rsqrt(var + BN_EPS)
            x = jax.nn.relu(gamma[l] * xn + beta[l])
        return x

    def _L0_ffn_ref(x, W_f, b_f, W_i, b_i, W_c, b_c, W_o, b_o):
        import jax, jax.numpy as jnp
        import numpy as np
        INPUT_SIZE = 512
        HIDDEN_SIZE = 512
        B, T, I = x.shape
        H = W_f.shape[1]
        h0 = jnp.zeros((B, H), dtype=x.dtype)
        c0 = jnp.zeros((B, H), dtype=x.dtype)

        def step(carry, x_t):
            h_prev, c_prev = carry
            combined = jnp.concatenate((x_t, h_prev), axis=1)
            f_t = jax.nn.sigmoid(combined @ W_f + b_f)
            i_t = jax.nn.sigmoid(combined @ W_i + b_i)
            c_tilde = jnp.tanh(combined @ W_c + b_c)
            c_t = f_t * c_prev + i_t * c_tilde
            o_t = jax.nn.sigmoid(combined @ W_o + b_o)
            h_t = o_t * jnp.tanh(c_t)
            return ((h_t, c_t), h_t)
        _, hs = jax.lax.scan(step, (h0, c0), jnp.swapaxes(x, 0, 1))
        return jnp.swapaxes(hs, 0, 1)
    edge_index = jnp.stack([src, dst])
    x = x + _L0_gnn_ref(_layernorm(x, axis=-1), L0_gnn_W, L0_gnn_b, L0_gnn_gamma, L0_gnn_beta, edge_index)
    x = x + _L0_ffn_ref(_layernorm(x, axis=-1)[None], L0_ffn_W_f, L0_ffn_b_f, L0_ffn_W_i, L0_ffn_b_i, L0_ffn_W_c, L0_ffn_b_c, L0_ffn_W_o, L0_ffn_b_o)[0]
    return x

_drawn_inputs = setup_inputs


def setup_inputs(seed=0):
    import zlib

    import numpy as np

    out = dict(_drawn_inputs(seed))
    spreads = {'L0_gnn_b': (0.0, 2.0), 'L0_gnn_gamma': (1.0, 0.2), 'L0_gnn_beta': (0.0, 0.1)}
    factors = {'L0_ffn_W_f': 5.902,
     'L0_ffn_b_f': 64.0,
     'L0_ffn_W_i': 3.584,
     'L0_ffn_b_i': 64.0,
     'L0_ffn_b_c': 8.0,
     'L0_ffn_W_o': 3.445,
     'L0_ffn_b_o': 64.0}
    for name, (base, spread) in spreads.items():
        noise = np.random.default_rng([zlib.crc32(name.encode()), seed]).standard_normal(out[name].shape)
        drawn = base * np.exp(spread * noise) if base else spread * noise
        out[name] = jnp.asarray(drawn.astype(out[name].dtype))
    for name, factor in factors.items():
        out[name] = (out[name] * factor).astype(out[name].dtype)
    return out
```

```python
import concourse.bass as bass
from concourse import mybir
from contextlib import ExitStack

FP32 = mybir.dt.float32
BF16 = mybir.dt.bfloat16
I32 = mybir.dt.int32
ALU = mybir.AluOpType
ACT = mybir.ActivationFunctionType
AX = mybir.AxisListType

P = 128
NODES = 10000
EDGES = 20000
D = 512
KT = D // P
LAYERS = 3
EPS = 1e-5
TILES = 80
ROWS = TILES * P
FULL_TILES = NODES // P
LAST_ROWS = NODES - FULL_TILES * P
FULL_EDGE_TILES = EDGES // P
LAST_EDGES = EDGES - FULL_EDGE_TILES * P
EDGE_TILES = 160
LAST_EDGE_TILE = FULL_EDGE_TILES
WINDOW = 3
GATES = 4


def hold(eng, sem, value, passed):
    eng.wait_ge(sem, value)
    eng.sem_inc(passed, 1)


def graph_tables(nc, dst, src, t):
    ctx = ExitStack()
    with ctx:
        def sb(name, shape, dt):
            return ctx.enter_context(nc.sbuf_tensor(name, shape, dt))

        def ps(name, shape, dt):
            return ctx.enter_context(nc.psum_tensor(name, shape, dt))

        def sem(name):
            return ctx.enter_context(nc.semaphore(name))

        BIG = 65536.0
        edge_rows = sb("edge_rows", [P, 4, P], I32)
        edge_f = sb("edge_f", [P, 4, P], FP32)
        dst_low = sb("dst_low", [P, EDGE_TILES], FP32)
        dst_high = sb("dst_high", [P, EDGE_TILES], FP32)
        dst_int = sb("dst_int", [P, EDGE_TILES], I32)
        part_int = sb("part_int", [P, EDGE_TILES], I32)
        iota_n = sb("iota_n", [P, TILES], FP32)
        tile_base = sb("tile_base", [P, TILES], FP32)
        low_hot = sb("low_hot", [P, 2, 8, P], BF16)
        high_hot = sb("high_hot", [P, 2, 8, TILES], BF16)
        zeros = sb("zeros", [P, P], BF16)
        no_pad = sb("no_pad", [P, 2, P], FP32)
        tile_max = sb("tile_max", [P, 2], FP32)
        tile_min = sb("tile_min", [P, 2], FP32)
        from_end = sb("from_end", [P, 2], FP32)
        from_start = sb("from_start", [P, 2], FP32)
        candidates = sb("candidates", [P, 4, TILES], FP32)
        reduced = sb("reduced", [P, 4, TILES], FP32)
        window_f = sb("window_f", [1, 4, TILES], FP32)
        degree = sb("degree", [P, TILES], FP32)
        turned = [ps(f"turned{i}", [P, P], FP32) for i in range(4)]
        degree_ps = ps("degree_ps", [P, TILES], FP32)

        padded = sem("gt_padded")
        edges_loaded = sem("gt_edges_loaded")
        consts = sem("gt_consts")
        floats = sem("gt_floats")
        transposed = sem("gt_transposed")
        tables = sem("gt_tables")
        hot = sem("gt_hot")
        counted = sem("gt_counted")
        cand = sem("gt_cand")
        maxed = sem("gt_maxed")
        rooted = sem("gt_rooted")
        v = sem("gt_vector_step")
        block = ctx.enter_context(nc.Block())

        @block.gpsimd
        def _(pool):
            nc.gpsimd.memset(edge_rows[:, 0:2, :], -1).then_inc(padded, 1)
            nc.gpsimd.memset(edge_rows[:, 2:4, :], 0).then_inc(padded, 1)
            nc.gpsimd.memset(zeros[:, :], 0.0).then_inc(consts, 1)
            nc.gpsimd.memset(t.ident[:, :], 0.0).then_inc(consts, 1)
            nc.gpsimd.iota(t.iota[:, :], pattern=[[1, P]], base=0, channel_multiplier=0,
                           allow_small_or_imprecise_dtypes=True).then_inc(consts, 1)
            nc.gpsimd.iota(iota_n[:, :], pattern=[[1, TILES]], base=0, channel_multiplier=0,
                           allow_small_or_imprecise_dtypes=True).then_inc(consts, 1)
            nc.gpsimd.iota(tile_base[:, :], pattern=[[P, TILES]], base=0, channel_multiplier=0,
                           allow_small_or_imprecise_dtypes=True).then_inc(consts, 1)
            nc.gpsimd.iota(from_end[:, :], pattern=[[-P, 2]], base=1000, channel_multiplier=-1,
                           allow_small_or_imprecise_dtypes=True).then_inc(consts, 1)
            nc.gpsimd.iota(from_start[:, :], pattern=[[P, 2]], base=1, channel_multiplier=1,
                           allow_small_or_imprecise_dtypes=True).then_inc(consts, 1)
            nc.gpsimd.memset(t.mask[:, :], 1.0).then_inc(consts, 1)
            pool.wait_ge(consts, 8)
            nc.gpsimd.affine_select(out=t.ident[:, :], in_=t.ident[:, :], compare_op=ALU.not_equal, fill=1.0,
                                    base=0, pattern=[[-1, P]], channel_multiplier=1).then_inc(consts, 1)
            nc.gpsimd.memset(t.mask[:, FULL_TILES:TILES], 0.0).then_inc(consts, 1)
            pool.wait_ge(consts, 10)
            nc.gpsimd.memset(t.mask[0:LAST_ROWS, FULL_TILES:FULL_TILES + 1], 1.0).then_inc(consts, 1)
            pool.wait_ge(cand, 4)
            nc.gpsimd.partition_all_reduce(reduced[:, :, :], candidates[:, :, :], P,
                                           bass.bass_isa.ReduceOp.max).then_inc(maxed, 1)

        @block.sync
        def _(sp):
            sp.wait_ge(padded, 2)
            for part, array in ((0, dst), (2, src)):
                rest = (FULL_EDGE_TILES - P)
                sp.dma_start(edge_rows[:, part, :],
                             array[0:P * P].rearrange("(j e) -> j e", e=P)).then_inc(edges_loaded, 16)
                sp.dma_start(edge_rows[0:rest, part + 1, :],
                             array[P * P:FULL_EDGE_TILES * P].rearrange("(j e) -> j e", e=P)).then_inc(edges_loaded, 16)
                sp.dma_start(edge_rows[rest:rest + 1, part + 1, 0:LAST_EDGES],
                             array[FULL_EDGE_TILES * P:EDGES].rearrange("(j e) -> j e", j=1)).then_inc(edges_loaded, 16)

        @block.vector
        def _(dve):
            steps = [0]

            def step(ins):
                steps[0] += 1
                ins.then_inc(v, 1)
                dve.wait_ge(v, steps[0])

            dve.wait_ge(edges_loaded, 96)
            nc.vector.tensor_copy(edge_f[:, :, :], edge_rows[:, :, :]).then_inc(floats, 1)
            dve.wait_ge(consts, 11)
            dve.wait_ge(floats, 1)
            rest = EDGE_TILES - P
            dve.wait_ge(transposed, 4)
            nc.vector.tensor_copy(t.dst_f[:, 0:P], turned[0][:, :])
            nc.vector.tensor_copy(t.dst_f[:, P:EDGE_TILES], turned[1][:, 0:rest])
            nc.vector.tensor_copy(dst_int[:, 0:P], turned[0][:, :])
            nc.vector.tensor_copy(dst_int[:, P:EDGE_TILES], turned[1][:, 0:rest])
            nc.vector.tensor_copy(t.src_i[:, 0:P], turned[2][:, :])
            step(nc.vector.tensor_copy(t.src_i[:, P:EDGE_TILES], turned[3][:, 0:rest]))
            step(nc.vector.tensor_scalar(part_int[:, :], dst_int[:, :], 127, None, ALU.bitwise_and))
            step(nc.vector.tensor_copy(dst_low[:, :], part_int[:, :]))
            step(nc.vector.tensor_scalar(part_int[:, :], dst_int[:, :], 7, None, ALU.arith_shift_right))
            step(nc.vector.tensor_copy(dst_high[:, :], part_int[:, :]))
            with dve.Fori(0, EDGE_TILES // 16) as i:
                for half in range(2):
                    first = i * 16 + half * 8
                    dve.wait_ge(counted, i * 2 + half + 1)
                    nc.vector.tensor_tensor(
                        low_hot[:, half, :, :], t.iota[:, :].unsqueeze(1).to_broadcast([P, 8, P]),
                        dst_low[:, bass.ds(first, 8)].unsqueeze(2).to_broadcast([P, 8, P]), ALU.is_equal).then_inc(hot, 1)
                    nc.vector.tensor_tensor(
                        high_hot[:, half, :, :], iota_n[:, :].unsqueeze(1).to_broadcast([P, 8, TILES]),
                        dst_high[:, bass.ds(first, 8)].unsqueeze(2).to_broadcast([P, 8, TILES]), ALU.is_equal).then_inc(hot, 1)
            dst_rows = edge_f[:, 0:2, :]
            nc.vector.tensor_reduce(tile_max[:, :], dst_rows, AX.X, ALU.max)
            step(nc.vector.tensor_scalar(no_pad[:, :, :], dst_rows, 0.0, BIG, ALU.is_lt, ALU.mult))
            step(nc.vector.tensor_tensor(no_pad[:, :, :], no_pad[:, :, :], dst_rows, ALU.add))
            step(nc.vector.tensor_reduce(tile_min[:, :], no_pad[:, :, :], AX.X, ALU.min))
            step(nc.vector.tensor_scalar(tile_min[:, :], tile_min[:, :], float(P), None, ALU.subtract))
            for g in range(2):
                nc.vector.tensor_scalar(candidates[:, g, :], tile_base[:, :], tile_max[:, g:g + 1],
                                        from_end[:, g:g + 1], ALU.is_le, ALU.mult).then_inc(cand, 1)
                nc.vector.tensor_scalar(candidates[:, 2 + g, :], tile_base[:, :], tile_min[:, g:g + 1],
                                        from_start[:, g:g + 1], ALU.is_gt, ALU.mult).then_inc(cand, 1)
            dve.wait_ge(maxed, 1)
            r = reduced[0:1, :, :]
            lo, hi, more = (window_f[:, k, :] for k in range(3))
            nc.vector.tensor_tensor(hi, r[:, 2, :], r[:, 3, :], ALU.max)
            step(nc.vector.tensor_tensor(lo, r[:, 0, :], r[:, 1, :], ALU.max))
            step(nc.vector.tensor_scalar(lo, lo, -1.0, 1000.0, ALU.mult, ALU.add))
            step(nc.vector.tensor_scalar(lo, lo, float(LAST_EDGE_TILE), None, ALU.min))
            step(nc.vector.tensor_tensor(more, hi, lo, ALU.subtract))
            step(nc.vector.tensor_scalar(more, more, float(WINDOW), 0.0, ALU.subtract, ALU.max))
            nc.vector.tensor_copy(t.first_edge_tile[:, :], lo).then_inc(tables, 1)
            nc.vector.tensor_copy(t.more_edge_tiles[:, :], more).then_inc(tables, 1)
            dve.wait_ge(counted, EDGE_TILES // 8 + 3)
            nc.vector.tensor_scalar(degree[:, :], degree_ps[:, :], 1.0, None, ALU.add).then_inc(tables, 1)
            dve.wait_ge(rooted, 1)
            nc.vector.memset(t.publish_scale[:, 2, :], 1.0)
            step(nc.vector.reciprocal(t.publish_scale[:, 0, :], degree[:, :]))
            step(nc.vector.tensor_copy(t.publish_scale[:, 1, :], t.publish_scale[:, 0, :]))
            nc.vector.tensor_scalar(t.node_base[:, :], tile_base[:, :], 0.0, None, ALU.add)
            nc.vector.memset(t.eps[:, :], EPS)
            dve.wait_ge(tables, 3)

        @block.scalar
        def _(act):
            act.wait_ge(tables, 3)
            nc.scalar.activation(degree[:, :], degree[:, :], ACT.Sqrt).then_inc(rooted, 1)

        @block.tensor
        def _(pe):
            pe.wait_ge(floats, 1)
            pe.wait_ge(consts, 11)
            for k in range(4):
                nc.tensor.transpose(turned[k][:, :], edge_f[:, k, :], t.ident[:, :]).then_inc(transposed, 1)
            nc.tensor.matmul(degree_ps[:, :], zeros[:, :], zeros[:, 0:TILES], start=True, stop=False)
            pe.sem_inc(counted, 2)
            with pe.Fori(0, EDGE_TILES // 16) as i:
                for half in range(2):
                    pe.wait_ge(hot, i * 4 + half * 2 + 2)
                    for k in range(8):
                        last = nc.tensor.matmul(degree_ps[:, :], low_hot[:, half, k, :], high_hot[:, half, k, :],
                                                start=False, stop=False)
                    last.then_inc(counted, 1)
            nc.tensor.matmul(degree_ps[:, :], zeros[:, :], zeros[:, 0:TILES], start=False, stop=True).then_inc(counted, 1)



def input_norm(nc, x, table, t):
    ctx = ExitStack()
    with ctx:
        def sb(name, shape, dt):
            return ctx.enter_context(nc.sbuf_tensor(name, shape, dt))

        def sem(name):
            return ctx.enter_context(nc.semaphore(name))

        RING = 4
        GROUPS = TILES // RING
        xin = sb("xin", [P, RING, D], FP32)
        out = sb("norm_out", [P, RING, D], FP32)
        stats = sb("norm_stats", [P, RING, 6], FP32)
        moments = sb("norm_moments", [P, RING, 2], FP32)
        std = sb("norm_std", [P, RING, 1], FP32)
        loaded = [sem(f"in_loaded{r}") for r in range(RING)]
        stored = [sem(f"in_stored{r}") for r in range(RING)]
        counted = sem("in_stats")
        averaged = sem("in_moments")
        rooted = sem("in_rooted")
        inverted = sem("in_inverted")
        normed = sem("in_normed")
        scaled = sem("in_scaled")
        passed = sem("in_passed")
        block = ctx.enter_context(nc.Block())

        @block.sync
        def _(sp):
            def load(n, r):
                sp.dma_start(xin[:, r, :], x[bass.ds(n * P, P), :]).then_inc(loaded[r], 16)

            def store(i, r):
                n = i * RING + r
                sp.wait_ge(scaled, n + 1)
                sp.dma_start(table[bass.ds(n * P, P), :], out[:, r, :]).then_inc(stored[r], 16)

            for r in range(RING):
                load(r, r)
                sp.sem_inc(stored[r], 16)
            with sp.Fori(0, GROUPS - 2) as i:
                for r in range(RING):
                    store(i, r)
                    sp.wait_ge(normed, i * RING + r + 1)
                    load((i + 1) * RING + r, r)
            for r in range(RING):
                n = (GROUPS - 1) * RING + r
                store(GROUPS - 2, r)
                sp.wait_ge(normed, (GROUPS - 2) * RING + r + 1)
                if n < FULL_TILES:
                    load(n, r)
                elif n == FULL_TILES:
                    sp.dma_start(xin[0:LAST_ROWS, r, :], x[FULL_TILES * P:NODES, :]).then_inc(loaded[r], 16)
                else:
                    sp.sem_inc(loaded[r], 16)
            for r in range(RING):
                store(GROUPS - 1, r)
            for r in range(RING):
                sp.wait_ge(stored[r], 16 * GROUPS + 16)

        @block.vector
        def _(dve):
            with dve.Fori(0, GROUPS) as i:
                for r in range(RING):
                    n = i * RING + r
                    dve.wait_ge(loaded[r], (i + 1) * 16)
                    nc.vector.bn_stats(stats[:, r, :], xin[:, r, :]).then_inc(counted, 1)
                    hold(dve, counted, n + 1, passed)
                    nc.vector.bn_aggr(moments[:, r, :], stats[:, r, :]).then_inc(averaged, 1)
                for r in range(RING):
                    n = i * RING + r
                    dve.wait_ge(rooted, n + 1)
                    nc.vector.reciprocal(std[:, r, :], std[:, r, :]).then_inc(inverted, 1)
                for r in range(RING):
                    n = i * RING + r
                    dve.wait_ge(inverted, n + 1)
                    nc.vector.tensor_scalar(t.rows[:, n, :], xin[:, r, :], moments[:, r, 0:1], std[:, r, :],
                                            ALU.subtract, ALU.mult).then_inc(normed, 1)

        @block.scalar
        def _(act):
            with act.Fori(0, GROUPS) as i:
                for r in range(RING):
                    n = i * RING + r
                    act.wait_ge(averaged, n + 1)
                    nc.scalar.activation(std[:, r, :], moments[:, r, 1:2], ACT.Sqrt, bias=t.eps[:, :]).then_inc(rooted, 1)
                for r in range(RING):
                    n = i * RING + r
                    act.wait_ge(stored[r], i * 16 + 16)
                    act.wait_ge(normed, n + 1)
                    nc.scalar.activation(out[:, r, :], t.rows[:, n, :], ACT.Copy,
                                         scale=t.publish_scale[:, 0, bass.ds(n, 1)]).then_inc(scaled, 1)


def beyond(nc, first, e):
    return nc.s_assert_within(first + e + WINDOW, min_val=WINDOW, max_val=EDGE_TILES - 1,
                              skip_runtime_bounds_check_because="more_edge_tiles counts up to LAST_EDGE_TILE")


def graph_layers(nc, table, W, b, gamma, beta, t):
    ctx = ExitStack()
    with ctx:
        def sb(name, shape, dt):
            return ctx.enter_context(nc.sbuf_tensor(name, shape, dt))

        def ps(name, shape, dt):
            return ctx.enter_context(nc.psum_tensor(name, shape, dt))

        def sem(name):
            return ctx.enter_context(nc.semaphore(name))

        PAIRS = TILES // 2
        STAGES = 4
        own = sb("own", [P, 2, D], FP32)
        gathered = sb("gathered", [P, 2, WINDOW, D], FP32)
        extra = sb("extra", [P, D], FP32)
        sources = sb("sources", [P, 2, WINDOW], I32)
        extra_source = sb("extra_source", [P, 1], I32)
        dst_in_tile = sb("dst_in_tile", [P, 2, WINDOW], FP32)
        extra_dst = sb("extra_dst", [P, 1], FP32)
        choose = sb("choose", [P, 2, WINDOW, P], FP32)
        extra_choose = sb("extra_choose", [P, P], FP32)
        summed = sb("summed", [P, 2, D], FP32)
        weights = sb("gnn_weights", [P, KT, D], FP32)
        weight_rows = gathered[:, :, :, :].rearrange("p q s d -> p (q s) d")[:, 0:KT, :]
        stage = gathered[:, :, :, :].rearrange("p q s d -> p (q s) d")[:, 0:STAGES, :]
        bias = sb("gnn_bias", [P, D], FP32)
        gamma_bc = sb("gamma_bc", [P, D], FP32)
        beta_bc = sb("beta_bc", [P, D], FP32)
        total = sb("total", [P, D], FP32)
        square = summed
        mean = bias
        ones = sb("ones", [P, P], FP32)

        sum_ps = [ps(f"sum_ps{q}", [P, D], FP32) for q in range(2)]
        z_ps = [ps(f"z_ps{q}", [P, D], FP32) for q in range(2)]
        turn_ps = [ps(f"turn_ps{q}", [P, D], FP32) for q in range(2)]
        mean_ps = ps("mean_ps", [P, D], FP32)
        square_ps = ps("square_ps", [P, D], FP32)

        table_stored = [sem(f"gl_table_stored{r}") for r in range(STAGES)]
        weights_loaded = sem("gl_weights_loaded")
        vectors_loaded = sem("gl_vectors_loaded")
        turned = sem("gl_weights_turned")
        weights_ready = sem("gl_weights_ready")
        source_ready = sem("gl_source_ready")
        fetched = [[sem(f"gl_fetched{q}{s}") for s in range(WINDOW)] for q in range(2)]
        own_ready = sem("gl_own_ready")
        dst_ready = sem("gl_dst_ready")
        choose_ready = sem("gl_choose_ready")
        sum_done = sem("gl_sum_done")
        sum_copied = sem("gl_sum_copied")
        z_done = sem("gl_z_done")
        z_read = sem("gl_z_read")
        total_done = sem("gl_total_done")
        x_source = sem("gl_extra_source")
        x_fetched = sem("gl_extra_fetched")
        x_dst = sem("gl_extra_dst")
        x_choose = sem("gl_extra_choose")
        x_used = sem("gl_extra_used")
        mean_done = sem("gl_mean_done")
        mean_ready = sem("gl_mean_ready")
        centred = sem("gl_centred")
        squared = sem("gl_squared")
        square_read = sem("gl_square_read")
        rooted = sem("gl_rooted")
        inverted = sem("gl_inverted")
        scale_ready = sem("gl_scale_ready")
        multiplied = sem("gl_multiplied")
        shifted = sem("gl_shifted")
        activated = sem("gl_activated")
        staged = sem("gl_staged")
        constant = sem("gl_ones")
        passed = sem("gl_passed")
        block = ctx.enter_context(nc.Block())

        @block.sync
        def _(sp):
            for r in range(STAGES):
                sp.sem_inc(table_stored[r], 16)
            sp.sem_inc(shifted, 1)
            with sp.Fori(0, LAYERS) as l:
                for r in range(STAGES):
                    sp.wait_ge(table_stored[r], l * (16 * TILES // STAGES) + 16)
                sp.dma_start(weight_rows[:, :, :],
                             W[bass.ds(l, 1), :, :].rearrange("l (k p) i -> p (l k) i", p=P)).then_inc(weights_loaded, 16)
                sp.wait_ge(shifted, l * TILES + 1)
                for array, place in ((b, bias), (gamma, gamma_bc), (beta, beta_bc)):
                    sp.dma_start(place[:, :], array[bass.ds(l, 1), :].to_broadcast([P, D])).then_inc(vectors_loaded, 16)
                with sp.Fori(0, TILES // STAGES) as i:
                    for r in range(STAGES):
                        n = i * STAGES + r
                        sp.wait_ge(staged, l * TILES + n + 1)
                        sp.dma_start(table[bass.ds(n * P, P), :], stage[:, r, :]).then_inc(table_stored[r], 16)
            for r in range(STAGES):
                sp.wait_ge(table_stored[r], 16 * LAYERS * TILES // STAGES + 16)

        @block.gpsimd
        def _(pool):
            nc.gpsimd.memset(ones[:, :], 1.0).then_inc(constant, 1)
            extras = pool.alloc_register("pool_extras")
            pool.reg_mov(extras, 0)
            with pool.Fori(0, LAYERS) as l:
                for r in range(STAGES):
                    pool.wait_ge(table_stored[r], l * (16 * TILES // STAGES) + 16)
                hold(pool, turned, l * KT + KT, passed)
                with pool.Fori(0, PAIRS) as i:
                    for q in range(2):
                        n = i * 2 + q
                        done = l * TILES + n
                        first = nc.gpsimd.value_load(t.first_edge_tile[0:1, bass.ds(n, 1)], min_val=0, max_val=LAST_EDGE_TILE)
                        pool.wait_ge(sum_done, done + 1)
                        nc.gpsimd.tensor_copy(sources[:, q, :], t.src_i[:, bass.ds(first, WINDOW)]).then_inc(source_ready, 1)
                        hold(pool, source_ready, done + 1, passed)
                        for s in range(WINDOW):
                            nc.gpsimd.indirect_dma_start(
                                out=gathered[:, q, s, :], out_offset=None, in_=table[:, :],
                                in_offset=bass.IndirectOffsetOnAxis(ap=sources[:, q, s:s + 1], axis=0),
                            ).then_inc(fetched[q][s], 16)
                        more = nc.gpsimd.value_load(t.more_edge_tiles[0:1, bass.ds(n, 1)], min_val=0, max_val=EDGE_TILES)
                        with pool.If(more > 0):
                            with pool.Fori(0, more) as e:
                                seen = pool.snap(extras)
                                pool.wait_ge(x_used, seen + 1)
                                nc.gpsimd.tensor_copy(extra_source[:, :],
                                                      t.src_i[:, bass.ds(beyond(nc, first, e), 1)]).then_inc(x_source, 1)
                                hold(pool, x_source, seen + 1, passed)
                                nc.gpsimd.indirect_dma_start(
                                    out=extra[:, :], out_offset=None, in_=table[:, :],
                                    in_offset=bass.IndirectOffsetOnAxis(ap=extra_source[:, 0:1], axis=0),
                                ).then_inc(x_fetched, 16)
                                pool.reg_add(extras, extras, 1)

        @block.vector
        def _(dve):
            extras = dve.alloc_register("dve_extras")
            dve.reg_mov(extras, 0)

            def build(l, n, q):
                done = l * TILES + n
                first = nc.vector.value_load(t.first_edge_tile[0:1, bass.ds(n, 1)], min_val=0, max_val=LAST_EDGE_TILE)
                more = nc.vector.value_load(t.more_edge_tiles[0:1, bass.ds(n, 1)], min_val=0, max_val=EDGE_TILES)
                dve.wait_ge(sum_done, done + 1)
                nc.vector.tensor_scalar(dst_in_tile[:, q, :], t.dst_f[:, bass.ds(first, WINDOW)],
                                        t.node_base[:, bass.ds(n, 1)], None, ALU.subtract).then_inc(dst_ready, 1)
                dve.wait_ge(dst_ready, done + 1)
                nc.vector.tensor_tensor(choose[:, q, :, :], t.iota[:, :].unsqueeze(1).to_broadcast([P, WINDOW, P]),
                                        dst_in_tile[:, q, :].unsqueeze(2).to_broadcast([P, WINDOW, P]),
                                        ALU.is_equal).then_inc(choose_ready, 1)
                with dve.If(more > 0):
                    with dve.Fori(0, more) as e:
                        seen = dve.snap(extras)
                        dve.wait_ge(x_used, seen + 1)
                        nc.vector.tensor_scalar(extra_dst[:, :], t.dst_f[:, bass.ds(beyond(nc, first, e), 1)],
                                                t.node_base[:, bass.ds(n, 1)], None, ALU.subtract).then_inc(x_dst, 1)
                        dve.wait_ge(x_dst, seen + 1)
                        nc.vector.tensor_scalar(extra_choose[:, :], t.iota[:, :], extra_dst[:, 0:1], None,
                                                ALU.is_equal).then_inc(x_choose, 1)
                        dve.reg_add(extras, extras, 1)

            def finish(l, n, q):
                done = l * TILES + n
                dve.wait_ge(z_done, done + 3)
                nc.vector.scalar_tensor_tensor(t.rows[:, n, :], z_ps[q][:, :], t.publish_scale[:, 0, bass.ds(n, 1)],
                                               bias[:, :], ALU.mult, ALU.add).then_inc(z_read, 1)
                dve.wait_ge(total_done, done + l + 1)
                dve.wait_ge(z_read, done + 3)
                nc.vector.scalar_tensor_tensor(total[:, :], t.rows[:, n, :], t.mask[:, bass.ds(n, 1)],
                                               total[:, :], ALU.mult, ALU.add).then_inc(total_done, 1)

            for q in range(2):
                dve.sem_inc(z_read, 1)
            with dve.Fori(0, LAYERS) as l:
                dve.wait_ge(vectors_loaded, l * 48 + 48)
                dve.wait_ge(mean_done, l + 1)
                nc.vector.memset(total[:, :], 0.0).then_inc(total_done, 1)
                build(l, 0, 0)
                build(l, 1, 1)
                with dve.Fori(0, PAIRS - 1) as i:
                    build(l, i * 2 + 2, 0)
                    finish(l, i * 2, 0)
                    build(l, i * 2 + 3, 1)
                    finish(l, i * 2 + 1, 1)
                finish(l, TILES - 2, 0)
                finish(l, TILES - 1, 1)
                dve.wait_ge(mean_done, l + 2)
                dve.wait_ge(z_read, l * TILES + TILES + 2)
                nc.vector.tensor_scalar(mean[:, :], mean_ps[:, :], 1.0 / NODES, None, ALU.mult).then_inc(mean_ready, 1)
                hold(dve, mean_ready, l + 1, passed)
                with dve.Fori(0, PAIRS) as i:
                    for q in range(2):
                        n = i * 2 + q
                        nc.vector.tensor_tensor(t.rows[:, n, :], t.rows[:, n, :], mean[:, :],
                                                ALU.subtract).then_inc(centred, 1)
                dve.wait_ge(rooted, l + 1)
                nc.vector.reciprocal(total[:, :], total[:, :]).then_inc(inverted, 1)
                dve.wait_ge(inverted, l + 1)
                nc.vector.tensor_tensor(gamma_bc[:, :], gamma_bc[:, :], total[:, :], ALU.mult).then_inc(scale_ready, 1)
                hold(dve, scale_ready, l + 1, passed)
                with dve.Fori(0, PAIRS) as i:
                    first = i * 2
                    done = l * TILES + first
                    for q in range(2):
                        nc.vector.tensor_tensor(t.rows[:, first + q, :], t.rows[:, first + q, :], gamma_bc[:, :],
                                                ALU.mult).then_inc(multiplied, 1)
                    for q in range(2):
                        dve.wait_ge(multiplied, done + q + 1)
                        nc.vector.tensor_tensor(t.rows[:, first + q, :], t.rows[:, first + q, :], beta_bc[:, :],
                                                ALU.add).then_inc(shifted, 1)

        @block.scalar
        def _(act):
            def scale_own(l, n, q):
                done = l * TILES + n
                act.wait_ge(sum_done, done + 1)
                nc.scalar.activation(own[:, q, :], t.rows[:, n, :], ACT.Copy,
                                     scale=t.publish_scale[:, 0, bass.ds(n, 1)]).then_inc(own_ready, 1)

            def copy_sum(l, n, q):
                done = l * TILES + n
                act.wait_ge(sum_done, done + 3)
                act.wait_ge(z_done, done + 1)
                nc.scalar.activation(summed[:, q, :], sum_ps[q][:, :], ACT.Copy).then_inc(sum_copied, 1)

            for q in range(2):
                act.sem_inc(sum_copied, 1)
            act.sem_inc(activated, 1)
            with act.Fori(0, LAYERS) as l:
                act.wait_ge(activated, l * TILES + 1)
                for k in range(KT):
                    act.wait_ge(turned, l * KT + k + 1)
                    nc.scalar.activation(weights[:, k, :], turn_ps[k % 2][:, :], ACT.Copy).then_inc(weights_ready, 1)
                scale_own(l, 0, 0)
                with act.Fori(0, PAIRS - 1) as i:
                    scale_own(l, i * 2 + 1, 1)
                    copy_sum(l, i * 2, 0)
                    scale_own(l, i * 2 + 2, 0)
                    copy_sum(l, i * 2 + 1, 1)
                scale_own(l, TILES - 1, 1)
                copy_sum(l, TILES - 2, 0)
                copy_sum(l, TILES - 1, 1)
                hold(act, z_done, l * TILES + TILES + 2, passed)
                with act.Fori(0, PAIRS) as i:
                    for q in range(2):
                        n = i * 2 + q
                        done = l * TILES + n
                        act.wait_ge(centred, done + 1)
                        act.wait_ge(square_read, done + 1)
                        nc.scalar.activation(square[:, q, :], t.rows[:, n, :], ACT.Square,
                                             scale=t.mask[:, bass.ds(n, 1)]).then_inc(squared, 1)
                act.wait_ge(square_read, l * TILES + TILES + 2)
                nc.scalar.activation(total[:, :], square_ps[:, :], ACT.Sqrt, bias=t.eps[:, :],
                                     scale=1.0 / NODES).then_inc(rooted, 1)
                with act.Fori(0, TILES // STAGES) as i:
                    for r in range(STAGES):
                        n = i * STAGES + r
                        act.wait_ge(shifted, l * TILES + n + 2)
                        nc.scalar.activation(t.rows[:, n, :], t.rows[:, n, :], ACT.Relu).then_inc(activated, 1)
                    for r in range(STAGES):
                        n = i * STAGES + r
                        act.wait_ge(activated, l * TILES + n + 2)
                        act.wait_ge(table_stored[r], l * (16 * TILES // STAGES) + i * 16 + 16)
                        nc.scalar.activation(stage[:, r, :], t.rows[:, n, :], ACT.Copy,
                                             scale=t.publish_scale[:, bass.ds(l + 0, 1), bass.ds(n, 1)]
                                             .rearrange("p a b -> p (a b)")).then_inc(staged, 1)

        @block.tensor
        def _(pe):
            extras = pe.alloc_register("pe_extras")
            pe.reg_mov(extras, 0)

            def sum_edges(l, i, q, n):
                done = l * TILES + n
                more = nc.tensor.value_load(t.more_edge_tiles[0:1, bass.ds(n, 1)], min_val=0, max_val=EDGE_TILES)
                pe.wait_ge(sum_copied, done + 1)
                pe.wait_ge(choose_ready, done + 1)
                for s in range(WINDOW):
                    pe.wait_ge(fetched[q][s], (l * PAIRS + i) * 16 + 16)
                    for k in range(KT):
                        nc.tensor.matmul(sum_ps[q][:, k * P:(k + 1) * P], gathered[:, q, s, k * P:(k + 1) * P],
                                         choose[:, q, s, :], start=(s == 0 and k == 0), stop=False,
                                         skip_group_check=True)
                with pe.If(more > 0):
                    with pe.Fori(0, more):
                        seen = pe.snap(extras)
                        pe.wait_ge(x_choose, seen + 1)
                        pe.wait_ge(x_fetched, seen * 16 + 16)
                        for k in range(KT):
                            last = nc.tensor.matmul(sum_ps[q][:, k * P:(k + 1) * P], extra[:, k * P:(k + 1) * P],
                                                    extra_choose[:, :], start=False, stop=False,
                                                    skip_group_check=True)
                        last.then_inc(x_used, 1)
                        pe.reg_add(extras, extras, 1)
                pe.wait_ge(own_ready, done + 1)
                for k in range(KT):
                    last = nc.tensor.matmul(sum_ps[q][:, k * P:(k + 1) * P], own[:, q, k * P:(k + 1) * P],
                                            t.ident[:, :], start=False, stop=True, skip_group_check=True)
                last.then_inc(sum_done, 1)

            def product(l, n, q):
                done = l * TILES + n
                pe.wait_ge(z_read, done + 1)
                pe.wait_ge(sum_copied, done + 3)
                for k in range(KT):
                    last = nc.tensor.matmul(z_ps[q][:, :], summed[:, q, k * P:(k + 1) * P], weights[:, k, :],
                                            start=(k == 0), stop=(k == KT - 1))
                last.then_inc(z_done, 1)

            pe.sem_inc(mean_done, 1)
            pe.sem_inc(x_used, 1)
            for q in range(2):
                pe.sem_inc(sum_done, 1)
                pe.sem_inc(z_done, 1)
                pe.sem_inc(square_read, 1)
            with pe.Fori(0, LAYERS) as l:
                pe.wait_ge(weights_loaded, l * 16 + 16)
                for k in range(KT):
                    if k >= 2:
                        pe.wait_ge(weights_ready, l * KT + k - 1)
                    for o in range(KT):
                        last = nc.tensor.transpose(turn_ps[k % 2][:, o * P:(o + 1) * P],
                                                   weight_rows[:, o, k * P:(k + 1) * P], t.ident[:, :])
                    last.then_inc(turned, 1)
                hold(pe, weights_ready, l * KT + KT, passed)
                sum_edges(l, 0, 0, 0)
                with pe.Fori(0, PAIRS - 1) as i:
                    sum_edges(l, i, 1, i * 2 + 1)
                    product(l, i * 2, 0)
                    sum_edges(l, i + 1, 0, i * 2 + 2)
                    product(l, i * 2 + 1, 1)
                sum_edges(l, PAIRS - 1, 1, TILES - 1)
                product(l, TILES - 2, 0)
                product(l, TILES - 1, 1)
                pe.wait_ge(constant, 1)
                pe.wait_ge(total_done, l * (TILES + 1) + TILES + 1)
                nc.tensor.matmul(mean_ps[:, :], ones[:, :], total[:, :], start=True, stop=True).then_inc(mean_done, 1)

                def add_square(i, q, start, stop):
                    pe.wait_ge(squared, l * TILES + i * 2 + q + 1)
                    return nc.tensor.matmul(square_ps[:, :], ones[:, :], square[:, q, :], start=start,
                                            stop=stop).then_inc(square_read, 1)

                add_square(0, 0, True, False)
                add_square(0, 1, False, False)
                with pe.Fori(1, PAIRS - 1) as i:
                    add_square(i, 0, False, False)
                    add_square(i, 1, False, False)
                add_square(PAIRS - 1, 0, False, False)
                add_square(PAIRS - 1, 1, False, True)


def gate_inputs(nc, x, table, residual, gate_in, w_gates, b_gates, t):
    ctx = ExitStack()
    with ctx:
        def sb(name, shape, dt):
            return ctx.enter_context(nc.sbuf_tensor(name, shape, dt))

        def ps(name, shape, dt):
            return ctx.enter_context(nc.psum_tensor(name, shape, dt))

        def sem(name):
            return ctx.enter_context(nc.semaphore(name))

        G = GATES * D
        weights = sb("input_weights", [P, KT, KT, GATES, P], FP32)
        bias = sb("gate_bias", [P, KT, GATES, P], FP32)
        xin = sb("gi_x", [P, 2, D], FP32)
        gnn = sb("gi_gnn", [P, 2, D], FP32)
        res = sb("gi_res", [P, 2, D], FP32)
        normed = sb("gi_normed", [P, 2, D], FP32)
        turned = sb("gi_turned", [P, 2, D], FP32)
        out = sb("gi_out", [P, 2, G], FP32)
        stats = sb("gi_stats", [P, 2, 6], FP32)
        moments = sb("gi_moments", [P, 2, 2], FP32)
        std = sb("gi_std", [P, 2, 1], FP32)
        gate_ps = [ps(f"gate_ps{j}", [P, D], FP32) for j in range(KT)]
        turn_ps = ps("gi_turn_ps", [P, D], FP32)

        weights_loaded = sem("gi_weights_loaded")
        x_loaded = [sem(f"gi_x_loaded{q}") for q in range(2)]
        gnn_loaded = [sem(f"gi_gnn_loaded{q}") for q in range(2)]
        res_stored = [sem(f"gi_res_stored{q}") for q in range(2)]
        out_stored = [sem(f"gi_out_stored{q}") for q in range(2)]
        out_free = [sem(f"gi_out_free{q}") for q in range(2)]
        res_ready = sem("gi_res_ready")
        counted = sem("gi_counted")
        passed = sem("gi_passed")
        averaged = sem("gi_averaged")
        rooted = sem("gi_rooted")
        inverted = sem("gi_inverted")
        norm_ready = sem("gi_norm_ready")
        turn_done = sem("gi_turn_done")
        turn_copied = sem("gi_turn_copied")
        gate_done = [sem(f"gi_gate_done{j}") for j in range(KT)]
        gate_read = [sem(f"gi_gate_read{j}") for j in range(KT)]
        block = ctx.enter_context(nc.Block())
        PAIRS = TILES // 2

        @block.sync
        def _(sp):
            def load(n, q):
                sp.dma_start(gnn[:, q, :], table[bass.ds(n * P, P), :]).then_inc(gnn_loaded[q], 16)
                sp.dma_start(xin[:, q, :], x[bass.ds(n * P, P), :]).then_inc(x_loaded[q], 16)

            def store(n, q):
                sp.wait_ge(res_ready, n + 1)
                sp.dma_start(residual[bass.ds(n * P, P), :], res[:, q, :]).then_inc(res_stored[q], 16)

            load(0, 0)
            load(1, 1)
            for q in range(2):
                sp.sem_inc(res_stored[q], 16)
            for g in range(GATES):
                for k in range(KT):
                    sp.dma_start(weights[:, k, :, g, :],
                                 w_gates[g][k * P:(k + 1) * P, :].rearrange("p (j u) -> p j u", u=P)
                                 ).then_inc(weights_loaded, 16)
                sp.dma_start(bias[:, :, g, :], b_gates[g].rearrange("(j u) -> j u", u=P).partition_broadcast(P)
                             ).then_inc(weights_loaded, 16)
            with sp.Fori(0, PAIRS - 2) as i:
                for q in range(2):
                    store(i * 2 + q, q)
                    load(i * 2 + q + 2, q)
            for q in range(2):
                n = FULL_TILES + q
                store(n - 2, q)
                sp.dma_start(gnn[:, q, :], table[n * P:(n + 1) * P, :]).then_inc(gnn_loaded[q], 16)
                if q == 0:
                    sp.dma_start(xin[0:LAST_ROWS, q, :], x[n * P:NODES, :]).then_inc(x_loaded[q], 16)
                else:
                    sp.sem_inc(x_loaded[q], 16)
            for q in range(2):
                store(FULL_TILES + q, q)
            for q in range(2):
                sp.wait_ge(res_stored[q], 16 * PAIRS + 16)

        @block.gpsimd
        def _(pool):
            with pool.Fori(0, PAIRS) as i:
                for q in range(2):
                    pool.wait_ge(gate_read[KT - 1], i * 2 + q + 2)
                    pool.dma_start(gate_in[bass.ds((i * 2 + q) * P, P), :], out[:, q, :]).then_inc(out_stored[q], 16)
                    pool.wait_ge(out_stored[q], i * 16 + 16)
                    pool.sem_inc(out_free[q], 1)

        @block.vector
        def _(dve):
            def norm(i, n, q):
                dve.wait_ge(x_loaded[q], i * 16 + 16)
                dve.wait_ge(gnn_loaded[q], i * 16 + 16)
                dve.wait_ge(res_stored[q], i * 16 + 16)
                nc.vector.tensor_tensor(res[:, q, :], xin[:, q, :], gnn[:, q, :], ALU.add).then_inc(res_ready, 1)
                dve.wait_ge(res_ready, n + 1)
                nc.vector.bn_stats(stats[:, q, :], res[:, q, :]).then_inc(counted, 1)
                hold(dve, counted, n + 1, passed)
                nc.vector.bn_aggr(moments[:, q, :], stats[:, q, :]).then_inc(averaged, 1)
                dve.wait_ge(rooted, n + 1)
                nc.vector.reciprocal(std[:, q, :], std[:, q, :]).then_inc(inverted, 1)
                dve.wait_ge(inverted, n + 1)
                nc.vector.tensor_scalar(normed[:, q, :], res[:, q, :], moments[:, q, 0:1], std[:, q, :],
                                        ALU.subtract, ALU.mult).then_inc(norm_ready, 1)

            def add_bias(i, n, q):
                dve.wait_ge(out_free[q], i + 1)
                for j in range(KT):
                    dve.wait_ge(gate_done[j], n + 1)
                    nc.vector.tensor_tensor(out[:, q, j * D:(j + 1) * D], gate_ps[j][:, :],
                                            bias[:, j, :, :].rearrange("p g u -> p (g u)"),
                                            ALU.add).then_inc(gate_read[j], 1)

            for j in range(KT):
                dve.sem_inc(gate_read[j], 1)
            for q in range(2):
                dve.sem_inc(out_free[q], 1)
            norm(0, 0, 0)
            dve.wait_ge(weights_loaded, 16 * GATES * (KT + 1))
            with dve.Fori(0, PAIRS - 1) as i:
                norm(i, i * 2 + 1, 1)
                add_bias(i, i * 2, 0)
                norm(i + 1, i * 2 + 2, 0)
                add_bias(i, i * 2 + 1, 1)
            norm(PAIRS - 1, TILES - 1, 1)
            add_bias(PAIRS - 1, TILES - 2, 0)
            add_bias(PAIRS - 1, TILES - 1, 1)

        @block.scalar
        def _(act):
            def serve(n, q):
                act.wait_ge(averaged, n + 1)
                nc.scalar.activation(std[:, q, :], moments[:, q, 1:2], ACT.Sqrt, bias=t.eps[:, :]).then_inc(rooted, 1)
                act.wait_ge(turn_done, n + 1)
                nc.scalar.activation(turned[:, q, :], turn_ps[:, :], ACT.Copy).then_inc(turn_copied, 1)

            act.sem_inc(turn_copied, 1)
            with act.Fori(0, PAIRS) as i:
                for q in range(2):
                    serve(i * 2 + q, q)

        @block.tensor
        def _(pe):
            def turn(n, q):
                pe.wait_ge(norm_ready, n + 1)
                pe.wait_ge(turn_copied, n + 1)
                for k in range(KT):
                    last = nc.tensor.transpose(turn_ps[:, k * P:(k + 1) * P], normed[:, q, k * P:(k + 1) * P],
                                               t.ident[:, :])
                last.then_inc(turn_done, 1)

            def product(n, q, j):
                pe.wait_ge(gate_read[j], n + 1)
                for k in range(KT):
                    last = nc.tensor.matmul(gate_ps[j][:, :], turned[:, q, k * P:(k + 1) * P],
                                            weights[:, k, j, :, :].rearrange("p g u -> p (g u)"),
                                            start=(k == 0), stop=(k == KT - 1))
                last.then_inc(gate_done[j], 1)

            def tile(n, q, more=True):
                pe.wait_ge(turn_copied, n + 2)
                product(n, q, 0)
                product(n, q, 1)
                if more:
                    turn(n + 1, 1 - q)
                product(n, q, 2)
                product(n, q, 3)

            turn(0, 0)
            pe.wait_ge(weights_loaded, 16 * GATES * (KT + 1))
            with pe.Fori(0, PAIRS - 1) as i:
                tile(i * 2, 0)
                tile(i * 2 + 1, 1)
            tile(TILES - 2, 0)
            tile(TILES - 1, 1, more=False)


def recurrence(nc, residual, gate_in, w_state, out, t):
    ctx = ExitStack()
    with ctx:
        def sb(name, shape, dt):
            return ctx.enter_context(nc.sbuf_tensor(name, shape, dt))

        def ps(name, shape, dt):
            return ctx.enter_context(nc.psum_tensor(name, shape, dt))

        def sem(name):
            return ctx.enter_context(nc.semaphore(name))

        STEPS = ROWS // P
        CHAINS = NODES // STEPS
        BLOCK = 10
        BLOCKS = STEPS // BLOCK
        CHECK_AT = 6
        TOLERANCE = 2.0 ** -20
        G = GATES * D
        C, H = 0, 1
        STORE_SPLIT = CHAINS // 16 * 16

        weights = sb("state_weights", [P, KT, KT, GATES, P], FP32)
        inputs = sb("inputs", [P, 2, G], FP32)
        res = sb("res", [P, 2, D], FP32)
        result = sb("result", [P, 2, D], FP32)
        before = sb("before", [P, KT, GATES, P], FP32)
        gates = sb("gates", [P, KT, GATES, P], FP32)
        state = sb("state", [P, 2, D], FP32)
        kept = sb("kept", [P, KT, P], FP32)
        added = sb("added", [P, KT, P], FP32)
        squashed = sb("squashed", [P, KT, P], FP32)
        h_turned = sb("h_turned", [P, KT, P], FP32)
        shift = sb("shift", [P, P], FP32)
        snap = sb("snap", [P, 2, D], FP32)
        history = sb("history", [P, BLOCKS, 2, D], FP32)
        change = sb("change", [P, 2, D], FP32)
        allowed = sb("allowed", [P, 2, D], FP32)
        excess = sb("excess", [P, 2, D], FP32)
        worst = sb("worst", [P, 1], FP32)
        worst_all = sb("worst_all", [P, 1], FP32)
        go_on = sb("go_on", [P, 1], I32)
        gate_ps = [ps(f"cell_ps{j}", [P, D], FP32) for j in range(KT)]
        turn_ps = [ps(f"cell_turn_ps{j}", [P, P], FP32) for j in range(KT)]

        weights_loaded = sem("re_weights_loaded")
        inputs_loaded = [sem(f"re_inputs_loaded{q}") for q in range(2)]
        res_loaded = [sem(f"re_res_loaded{q}") for q in range(2)]
        stored = [sem(f"re_stored{q}") for q in range(2)]
        shift_zero = sem("re_shift_zero")
        shift_ready = sem("re_shift_ready")
        history_ready = sem("re_history_ready")
        gate_done = [sem(f"re_gate_done{j}") for j in range(KT)]
        gate_read = [sem(f"re_gate_read{j}") for j in range(KT)]
        gates_ready = [sem(f"re_gates_ready{j}") for j in range(KT)]
        product_ready = [sem(f"re_product_ready{j}") for j in range(KT)]
        c_ready = [sem(f"re_c_ready{j}") for j in range(KT)]
        squash_ready = [sem(f"re_squash_ready{j}") for j in range(KT)]
        h_ready = [sem(f"re_h_ready{j}") for j in range(KT)]
        turned = [sem(f"re_turned{j}") for j in range(KT)]
        copied = [sem(f"re_copied{j}") for j in range(KT)]
        moved = sem("re_moved")
        c_moved = sem("re_c_moved")
        result_ready = sem("re_result_ready")
        snapped = sem("re_snapped")
        check = sem("re_check")
        excess_ready = sem("re_excess_ready")
        worst_ready = sem("re_worst_ready")
        worst_shared = sem("re_worst_shared")
        flag_ready = sem("re_flag_ready")
        flag_seen = sem("re_flag_seen")
        passed = sem("re_passed")
        block_ = ctx.enter_context(nc.Block())

        by_step_in = gate_in.rearrange("(c t) f -> t c f", t=STEPS)
        by_step_res = residual.rearrange("(c t) f -> t c f", t=STEPS)
        by_step_out = out.rearrange("(c t) f -> t c f", t=STEPS)

        def uses(done, pair):
            return done * (BLOCK // 2) + pair

        def sweeps(eng, begin, step):
            go = eng.alloc_register("go")
            eng.reg_mov(go, 1)
            with eng.Fori(0, CHAINS) as sweep:
                with eng.If(eng.snap(go) > 0):
                    begin(sweep, sweep * STEPS)
                    with eng.Fori(0, BLOCKS) as b:
                        with eng.If(eng.snap(go) > 0):
                            done = sweep * BLOCKS + b
                            with eng.Fori(0, CHECK_AT // 2) as u:
                                for q in range(2):
                                    step(sweep, done, b, u, u * 2 + q, q)
                            for k in range(CHECK_AT, BLOCK):
                                step(sweep, done, b, k // 2, k, k % 2)
                            hold(eng, flag_ready, done + 1, passed)
                            eng.reg_load(go, go_on[0:1, 0:1]).then_inc(flag_seen, 1)
                        eng.sem_inc(passed, 1)
                eng.sem_inc(passed, 1)

        @block_.sync
        def _(sp):
            def load_inputs(tile, q):
                sp.dma_start(inputs[:, q, :], by_step_in[bass.ds(tile, 1), :, :].rearrange("t c f -> c (t f)")
                             ).then_inc(inputs_loaded[q], 16)

            def load_res(tile, q):
                sp.dma_start(res[:, q, :], by_step_res[bass.ds(tile, 1), :, :].rearrange("t c f -> c (t f)")
                             ).then_inc(res_loaded[q], 16)

            def begin(sweep, steps):
                pass

            def step(sweep, done, b, pair, k, q):
                count = done * BLOCK + k
                ahead = (b * BLOCK + k + 2) % STEPS
                sp.wait_ge(gate_read[KT - 1], count + 2)
                load_inputs(ahead, q)
                sp.wait_ge(result_ready, count + 2)
                tile = b * BLOCK + k
                for a, z in ((0, STORE_SPLIT), (STORE_SPLIT, CHAINS)):
                    sp.dma_start(by_step_out[bass.ds(tile, 1), a:z, :].rearrange("t c f -> c (t f)"),
                                 result[a:z, q, :]).then_inc(stored[q], 16)
                load_res(ahead, q)

            for q in range(2):
                load_inputs(q, q)
                load_res(q, q)
                sp.sem_inc(stored[q], 32)
            for g in range(GATES):
                for k in range(KT):
                    sp.dma_start(weights[:, k, :, g, :],
                                 w_state[g][k * P:(k + 1) * P, :].rearrange("p (j u) -> p j u", u=P)
                                 ).then_inc(weights_loaded, 16)
            blocks = sp.alloc_register("blocks_run")
            sp.reg_mov(blocks, 0)

            def counted_step(sweep, done, b, pair, k, q):
                step(sweep, done, b, pair, k, q)
                if isinstance(k, int) and k == BLOCK - 1:
                    sp.reg_add(blocks, blocks, 1)

            sweeps(sp, begin, counted_step)
            ran = sp.snap(blocks)
            for q in range(2):
                hold(sp, stored[q], ran * (BLOCK * 16) + 32, passed)
                hold(sp, inputs_loaded[q], ran * (BLOCK * 8) + 16, passed)
                hold(sp, res_loaded[q], ran * (BLOCK * 8) + 16, passed)

        @block_.gpsimd
        def _(pool):
            nc.gpsimd.memset(shift[:, :], 0.0).then_inc(shift_zero, 1)
            pool.wait_ge(shift_zero, 1)
            nc.gpsimd.affine_select(out=shift[:, :], in_=shift[:, :], compare_op=ALU.not_equal, fill=1.0, base=1,
                                    pattern=[[-1, P]], channel_multiplier=1).then_inc(shift_ready, 1)
            nc.gpsimd.memset(history[:, :, :, :], 1e15).then_inc(history_ready, 1)
            nc.gpsimd.memset(excess[:, :, :], -1.0).then_inc(history_ready, 1)
            pool.wait_ge(history_ready, 2)

            def begin(sweep, steps):
                pass

            def step(sweep, done, b, pair, k, q):
                count = done * BLOCK + k
                half = done * (BLOCK // 2) + k // 2 if isinstance(k, int) else None
                pool.wait_ge(res_loaded[q], uses(done, pair) * 16 + 16)
                pool.wait_ge(stored[q], uses(done, pair) * 32 + 32)
                hold(pool, h_ready[KT - 1], count + sweep + 3, passed)
                nc.gpsimd.tensor_tensor(result[:, q, :], state[:, H, :], res[:, q, :], ALU.add).then_inc(result_ready, 1)
                if isinstance(k, int) and k == CHECK_AT:
                    rows = slice(0, CHAINS)
                    old = history[rows, bass.ds(b, 1), :, :].rearrange("p b s d -> p (b s) d")
                    pool.wait_ge(snapped, done + 1)
                    nc.gpsimd.tensor_tensor(change[rows], snap[rows], old, ALU.subtract)
                    nc.gpsimd.tensor_tensor(allowed[rows], snap[rows], snap[rows], ALU.mult).then_inc(check, 1)
                    pool.wait_ge(check, done * 4 + 2)
                    nc.gpsimd.tensor_tensor(change[rows], change[rows], change[rows], ALU.mult)
                    nc.gpsimd.tensor_scalar(allowed[rows], allowed[rows], 1.0, TOLERANCE * TOLERANCE, ALU.max,
                                            ALU.mult).then_inc(check, 1)
                    pool.wait_ge(check, done * 4 + 3)
                    nc.gpsimd.tensor_tensor(excess[rows], change[rows], allowed[rows], ALU.subtract
                                            ).then_inc(excess_ready, 1)
                    nc.gpsimd.tensor_copy(old, snap[rows]).then_inc(check, 2)
                if isinstance(k, int) and k == BLOCK - 1:
                    hold(pool, worst_ready, done + 1, passed)
                    nc.gpsimd.partition_all_reduce(worst_all[:, :], worst[:, :], P,
                                                   bass.bass_isa.ReduceOp.max).then_inc(worst_shared, 1)
                    pool.wait_ge(worst_shared, done + 1)
                    hold(pool, flag_seen, done * 5 + 1, passed)
                    nc.gpsimd.tensor_scalar(go_on[:, :], worst_all[:, :], 0.0, None, ALU.is_gt).then_inc(flag_ready, 1)

            pool.sem_inc(result_ready, 1)
            pool.sem_inc(flag_seen, 1)
            pool.sem_inc(check, 1)
            sweeps(pool, begin, step)

        @block_.vector
        def _(dve):
            nc.vector.memset(state[:, C, :], 0.0)
            for j in range(KT):
                nc.vector.memset(state[:, H, j * P:(j + 1) * P], 0.0).then_inc(h_ready[j], 1)
            for j in range(KT):
                dve.sem_inc(gate_read[j], 1)

            def begin(sweep, steps):
                dve.wait_ge(moved, sweep * 2 + 1)
                nc.vector.tensor_copy(state[:, C, :], gate_ps[0][:, :]).then_inc(c_moved, 1)
                dve.wait_ge(moved, sweep * 2 + 2)
                dve.wait_ge(result_ready, steps + 1)
                for j in range(KT):
                    nc.vector.tensor_copy(state[:, H, j * P:(j + 1) * P],
                                          gate_ps[1][:, j * P:(j + 1) * P]).then_inc(h_ready[j], 1)
                hold(dve, c_moved, sweep + 1, passed)

            def step(sweep, done, b, pair, k, q):
                count = done * BLOCK + k

                def add(j):
                    if j == 0:
                        dve.wait_ge(inputs_loaded[q], uses(done, pair) * 16 + 16)
                    dve.wait_ge(gate_done[j], count + 1)
                    nc.vector.tensor_tensor(before[:, j, :, :].rearrange("p g u -> p (g u)"), gate_ps[j][:, :],
                                            inputs[:, q, j * D:(j + 1) * D], ALU.add).then_inc(gate_read[j], 1)

                def update(j):
                    c = state[:, C, j * P:(j + 1) * P]
                    dve.wait_ge(gates_ready[j], count * 2 + 2)
                    nc.vector.tensor_tensor(kept[:, j, :], gates[:, j, 0, :], c, ALU.mult)
                    nc.vector.tensor_tensor(added[:, j, :], gates[:, j, 1, :], gates[:, j, 3, :],
                                            ALU.mult).then_inc(product_ready[j], 1)
                    dve.wait_ge(product_ready[j], count + 1)
                    nc.vector.tensor_tensor(c, kept[:, j, :], added[:, j, :], ALU.add).then_inc(c_ready[j], 1)

                def output(j):
                    if j == 0:
                        dve.wait_ge(result_ready, count + 1)
                    dve.wait_ge(squash_ready[j], count + 1)
                    nc.vector.tensor_tensor(state[:, H, j * P:(j + 1) * P], gates[:, j, 2, :], squashed[:, j, :],
                                            ALU.mult).then_inc(h_ready[j], 1)

                if isinstance(k, int) and k == BLOCK - 1:
                    dve.wait_ge(excess_ready, done + 1)
                    nc.vector.tensor_reduce(worst[:, :], excess[:, :, :], AX.XY, ALU.max).then_inc(worst_ready, 1)
                add(0)
                update(0)
                add(1)
                output(0)
                update(1)
                add(2)
                output(1)
                update(2)
                add(3)
                output(2)
                update(3)
                output(3)

            dve.wait_ge(history_ready, 2)
            sweeps(dve, begin, step)

        @block_.scalar
        def _(act):
            def copy_h(j, value):
                act.wait_ge(turned[j], value)
                nc.scalar.activation(h_turned[:, j, :], turn_ps[j][:, :], ACT.Copy).then_inc(copied[j], 1)

            def begin(sweep, steps):
                copy_h(0, steps + sweep + 1)

            def step(sweep, done, b, pair, k, q):
                count = done * BLOCK + k

                def activate(j):
                    act.wait_ge(gate_read[j], count + 2)
                    nc.scalar.activation(gates[:, j, 0:3, :], before[:, j, 0:3, :], ACT.Sigmoid
                                         ).then_inc(gates_ready[j], 1)
                    nc.scalar.activation(gates[:, j, 3, :], before[:, j, 3, :], ACT.Tanh).then_inc(gates_ready[j], 1)

                def squash(j):
                    act.wait_ge(c_ready[j], count + 1)
                    nc.scalar.activation(squashed[:, j, :], state[:, C, j * P:(j + 1) * P], ACT.Tanh
                                         ).then_inc(squash_ready[j], 1)

                for j in range(1, KT):
                    copy_h(j, count + 1)
                for j in range(KT):
                    if j == KT - 1:
                        copy_h(0, count + sweep + 2)
                    activate(j)
                    squash(j)
                if isinstance(k, int) and k == CHECK_AT:
                    act.wait_ge(h_ready[KT - 1], count + sweep + 3)
                    act.wait_ge(check, done * 4 + 1)
                    nc.scalar.activation(snap[:, :, :], state[:, :, :], ACT.Copy).then_inc(snapped, 1)

            sweeps(act, begin, step)

        @block_.tensor
        def _(pe):
            def turn(j, h_count):
                pe.wait_ge(h_ready[j], h_count)
                nc.tensor.transpose(turn_ps[j][:, :], state[:, H, j * P:(j + 1) * P], t.ident[:, :]
                                    ).then_inc(turned[j], 1)

            def begin(sweep, steps):
                pe.wait_ge(h_ready[KT - 1], steps + sweep + 1)
                nc.tensor.matmul(gate_ps[0][:, :], shift[:, :], state[:, C, :], start=True, stop=True
                                 ).then_inc(moved, 1)
                nc.tensor.matmul(gate_ps[1][:, :], shift[:, :], state[:, H, :], start=True, stop=True
                                 ).then_inc(moved, 1)
                turn(0, steps + sweep + 2)
                pe.wait_ge(c_moved, sweep + 1)
                hold(pe, h_ready[KT - 1], steps + sweep + 2, passed)

            def step(sweep, done, b, pair, k, q):
                count = done * BLOCK + k

                def part(j, kt):
                    if kt == 0:
                        pe.wait_ge(gate_read[j], count + 1)
                    return nc.tensor.matmul(gate_ps[j][:, :], h_turned[:, kt, :],
                                            weights[:, kt, j, :, :].rearrange("p g u -> p (g u)"),
                                            start=(kt == 0), stop=(kt == KT - 1))

                def turn_last(j):
                    turn(j, count + sweep + 2)

                pe.wait_ge(copied[0], count + sweep + 1)
                part(0, 0)
                part(1, 0)
                turn_last(1)
                part(2, 0)
                part(3, 0)
                pe.wait_ge(copied[1], count + 1)
                part(0, 1)
                turn_last(2)
                part(1, 1)
                part(2, 1)
                turn_last(3)
                part(3, 1)
                pe.wait_ge(copied[2], count + 1)
                for j in range(KT):
                    part(j, 2)
                    if j == 0:
                        pe.wait_ge(copied[3], count + 1)
                    if j == KT - 1:
                        turn(0, count + sweep + 3)
                    part(j, 3).then_inc(gate_done[j], 1)

            pe.wait_ge(shift_ready, 1)
            pe.wait_ge(weights_loaded, 16 * GATES * KT)
            sweeps(pe, begin, step)


class Tables:
    pass


def gnn_lstm(nc, x, src, dst, W, b, gamma, beta, w_gates, b_gates, out):
    table = nc.dram_tensor("table", [ROWS, D], FP32, kind="Internal").ap()
    residual = nc.dram_tensor("residual", [ROWS, D], FP32, kind="Internal").ap()
    gate_in = nc.dram_tensor("gate_in", [ROWS, GATES * D], FP32, kind="Internal").ap()
    w_in = [w[0:D, :] for w in w_gates]
    w_state = [w[D:2 * D, :] for w in w_gates]
    ctx = ExitStack()
    with ctx:
        def sb(name, shape, dt):
            return ctx.enter_context(nc.sbuf_tensor(name, shape, dt))

        t = Tables()
        t.ident = sb("ident", [P, P], FP32)
        t.iota = sb("iota", [P, P], FP32)
        t.eps = sb("eps", [P, 1], FP32)
        with ExitStack() as graph:
            def gsb(name, shape, dt):
                return graph.enter_context(nc.sbuf_tensor(name, shape, dt))

            t.dst_f = gsb("dst_f", [P, EDGE_TILES], FP32)
            t.src_i = gsb("src_i", [P, EDGE_TILES], I32)
            t.node_base = gsb("node_base", [P, TILES], FP32)
            t.mask = gsb("mask", [P, TILES], FP32)
            t.publish_scale = gsb("publish_scale", [P, LAYERS, TILES], FP32)
            t.first_edge_tile = gsb("first_edge_tile", [1, TILES], I32)
            t.more_edge_tiles = gsb("more_edge_tiles", [1, TILES], I32)
            graph_tables(nc, dst, src, t)
            t.rows = gsb("rows", [P, TILES, D], FP32)
            input_norm(nc, x, table, t)
            graph_layers(nc, table, W, b, gamma, beta, t)
        gate_inputs(nc, x, table, residual, gate_in, w_in, b_gates, t)
        recurrence(nc, residual, gate_in, w_state, out, t)


def kernel(x, src, dst, L0_gnn_W, L0_gnn_b, L0_gnn_gamma, L0_gnn_beta, L0_ffn_W_f, L0_ffn_b_f, L0_ffn_W_i,
           L0_ffn_b_i, L0_ffn_W_c, L0_ffn_b_c, L0_ffn_W_o, L0_ffn_b_o):
    import numpy as _np
    import concourse.bacc as _bacc
    from concourse import mybir as _mybir
    from concourse.bass_utils import run_bass_kernel_spmd as _run

    nc = _bacc.Bacc("TRN2", target_bir_lowering=False, num_devices=1)
    arrays = {
        "x": x, "src": src, "dst": dst, "gnn_w": L0_gnn_W, "gnn_b": L0_gnn_b, "gnn_gamma": L0_gnn_gamma,
        "gnn_beta": L0_gnn_beta, "w_f": L0_ffn_W_f, "w_i": L0_ffn_W_i, "w_o": L0_ffn_W_o, "w_c": L0_ffn_W_c,
        "b_f": L0_ffn_b_f, "b_i": L0_ffn_b_i, "b_o": L0_ffn_b_o, "b_c": L0_ffn_b_c,
    }
    arrays = {name: _np.ascontiguousarray(a) for name, a in arrays.items()}
    d = {name: nc.dram_tensor(f"{name}_in", a.shape, _mybir.dt.from_np(a.dtype), kind="ExternalInput").ap()
         for name, a in arrays.items()}
    out = nc.dram_tensor("out", [NODES, D], FP32, kind="ExternalOutput").ap()
    gnn_lstm(nc, d["x"], d["src"], d["dst"], d["gnn_w"], d["gnn_b"], d["gnn_gamma"], d["gnn_beta"],
             [d["w_f"], d["w_i"], d["w_o"], d["w_c"]], [d["b_f"], d["b_i"], d["b_o"], d["b_c"]], out)
    r = _run(nc, [{f"{name}_in": a for name, a in arrays.items()}], core_ids=[0])
    return r.results[0]["out"]
```

```python
import concourse.bass as bass
from concourse import mybir
from contextlib import ExitStack

FP32 = mybir.dt.float32
FP32R = mybir.dt.float32r
BF16 = mybir.dt.bfloat16
I32 = mybir.dt.int32
ALU = mybir.AluOpType
ACT = mybir.ActivationFunctionType
AX = mybir.AxisListType

P = 128
NODES = 10000
EDGES = 20000
D = 512
KT = D // P
LAYERS = 3
EPS = 1e-5
TILES = 80
ROWS = TILES * P
FULL_TILES = NODES // P
LAST_ROWS = NODES - FULL_TILES * P
FULL_EDGE_TILES = EDGES // P
LAST_EDGES = EDGES - FULL_EDGE_TILES * P
EDGE_TILES = 160
LAST_EDGE_TILE = FULL_EDGE_TILES
WINDOW = 3
GATES = 4


def hold(eng, sem, value, passed):
    eng.wait_ge(sem, value)
    eng.sem_inc(passed, 1)


def graph_tables(nc, dst, src, t):
    ctx = ExitStack()
    with ctx:
        def sb(name, shape, dt):
            return ctx.enter_context(nc.sbuf_tensor(name, shape, dt))

        def ps(name, shape, dt):
            return ctx.enter_context(nc.psum_tensor(name, shape, dt))

        def sem(name):
            return ctx.enter_context(nc.semaphore(name))

        BIG = 65536.0
        edge_rows = sb("edge_rows", [P, 4, P], I32)
        edge_f = sb("edge_f", [P, 4, P], FP32)
        dst_low = sb("dst_low", [P, EDGE_TILES], FP32)
        dst_high = sb("dst_high", [P, EDGE_TILES], FP32)
        dst_int = sb("dst_int", [P, EDGE_TILES], I32)
        part_int = sb("part_int", [P, EDGE_TILES], I32)
        iota_n = sb("iota_n", [P, TILES], FP32)
        tile_base = sb("tile_base", [P, TILES], FP32)
        low_hot = sb("low_hot", [P, 2, 8, P], BF16)
        high_hot = sb("high_hot", [P, 2, 8, TILES], BF16)
        zeros = sb("zeros", [P, P], BF16)
        no_pad = sb("no_pad", [P, 2, P], FP32)
        tile_max = sb("tile_max", [P, 2], FP32)
        tile_min = sb("tile_min", [P, 2], FP32)
        from_end = sb("from_end", [P, 2], FP32)
        from_start = sb("from_start", [P, 2], FP32)
        candidates = sb("candidates", [P, 4, TILES], FP32)
        reduced = sb("reduced", [P, 4, TILES], FP32)
        window_f = sb("window_f", [1, 4, TILES], FP32)
        degree = sb("degree", [P, TILES], FP32)
        turned = [ps(f"turned{i}", [P, P], FP32) for i in range(4)]
        degree_ps = ps("degree_ps", [P, TILES], FP32)

        padded = sem("gt_padded")
        edges_loaded = sem("gt_edges_loaded")
        consts = sem("gt_consts")
        floats = sem("gt_floats")
        transposed = sem("gt_transposed")
        tables = sem("gt_tables")
        hot = sem("gt_hot")
        counted = sem("gt_counted")
        cand = sem("gt_cand")
        maxed = sem("gt_maxed")
        rooted = sem("gt_rooted")
        v = sem("gt_vector_step")
        block = ctx.enter_context(nc.Block())

        @block.gpsimd
        def _(pool):
            nc.gpsimd.memset(edge_rows[:, 0:2, :], -1).then_inc(padded, 1)
            nc.gpsimd.memset(edge_rows[:, 2:4, :], 0).then_inc(padded, 1)
            nc.gpsimd.memset(zeros[:, :], 0.0).then_inc(consts, 1)
            nc.gpsimd.memset(t.ident[:, :], 0.0).then_inc(consts, 1)
            nc.gpsimd.iota(t.iota[:, :], pattern=[[1, P]], base=0, channel_multiplier=0,
                           allow_small_or_imprecise_dtypes=True).then_inc(consts, 1)
            nc.gpsimd.iota(iota_n[:, :], pattern=[[1, TILES]], base=0, channel_multiplier=0,
                           allow_small_or_imprecise_dtypes=True).then_inc(consts, 1)
            nc.gpsimd.iota(tile_base[:, :], pattern=[[P, TILES]], base=0, channel_multiplier=0,
                           allow_small_or_imprecise_dtypes=True).then_inc(consts, 1)
            nc.gpsimd.iota(from_end[:, :], pattern=[[-P, 2]], base=1000, channel_multiplier=-1,
                           allow_small_or_imprecise_dtypes=True).then_inc(consts, 1)
            nc.gpsimd.iota(from_start[:, :], pattern=[[P, 2]], base=1, channel_multiplier=1,
                           allow_small_or_imprecise_dtypes=True).then_inc(consts, 1)
            nc.gpsimd.memset(t.mask[:, :], 0.0).then_inc(consts, 1)
            pool.wait_ge(consts, 8)
            nc.gpsimd.affine_select(out=t.ident[:, :], in_=t.ident[:, :], compare_op=ALU.not_equal, fill=1.0,
                                    base=0, pattern=[[-1, P]], channel_multiplier=1).then_inc(consts, 1)
            nc.gpsimd.memset(t.mask[0:LAST_ROWS, 0:1], 1.0).then_inc(consts, 1)
            pool.wait_ge(cand, 4)
            nc.gpsimd.partition_all_reduce(reduced[:, :, :], candidates[:, :, :], P,
                                           bass.bass_isa.ReduceOp.max).then_inc(maxed, 1)

        @block.sync
        def _(sp):
            sp.wait_ge(padded, 2)
            for part, array in ((0, dst), (2, src)):
                rest = (FULL_EDGE_TILES - P)
                sp.dma_start(edge_rows[:, part, :],
                             array[0:P * P].rearrange("(j e) -> j e", e=P)).then_inc(edges_loaded, 16)
                sp.dma_start(edge_rows[0:rest, part + 1, :],
                             array[P * P:FULL_EDGE_TILES * P].rearrange("(j e) -> j e", e=P)).then_inc(edges_loaded, 16)
                sp.dma_start(edge_rows[rest:rest + 1, part + 1, 0:LAST_EDGES],
                             array[FULL_EDGE_TILES * P:EDGES].rearrange("(j e) -> j e", j=1)).then_inc(edges_loaded, 16)

        @block.vector
        def _(dve):
            steps = [0]

            def step(ins):
                steps[0] += 1
                ins.then_inc(v, 1)
                dve.wait_ge(v, steps[0])

            dve.wait_ge(edges_loaded, 96)
            nc.vector.tensor_copy(edge_f[:, :, :], edge_rows[:, :, :]).then_inc(floats, 1)
            dve.wait_ge(consts, 10)
            dve.wait_ge(floats, 1)
            rest = EDGE_TILES - P
            dve.wait_ge(transposed, 4)
            nc.vector.tensor_copy(t.dst_f[:, 0:P], turned[0][:, :])
            nc.vector.tensor_copy(t.dst_f[:, P:EDGE_TILES], turned[1][:, 0:rest])
            nc.vector.tensor_copy(dst_int[:, 0:P], turned[0][:, :])
            nc.vector.tensor_copy(dst_int[:, P:EDGE_TILES], turned[1][:, 0:rest])
            nc.vector.tensor_copy(t.src_i[:, 0:P], turned[2][:, :])
            step(nc.vector.tensor_copy(t.src_i[:, P:EDGE_TILES], turned[3][:, 0:rest]))
            step(nc.vector.tensor_scalar(part_int[:, :], dst_int[:, :], 127, None, ALU.bitwise_and))
            step(nc.vector.tensor_copy(dst_low[:, :], part_int[:, :]))
            step(nc.vector.tensor_scalar(part_int[:, :], dst_int[:, :], 7, None, ALU.arith_shift_right))
            step(nc.vector.tensor_copy(dst_high[:, :], part_int[:, :]))
            with dve.Fori(0, EDGE_TILES // 16) as i:
                for half in range(2):
                    first = i * 16 + half * 8
                    dve.wait_ge(counted, i * 2 + half + 1)
                    nc.vector.tensor_tensor(
                        low_hot[:, half, :, :], t.iota[:, :].unsqueeze(1).to_broadcast([P, 8, P]),
                        dst_low[:, bass.ds(first, 8)].unsqueeze(2).to_broadcast([P, 8, P]), ALU.is_equal).then_inc(hot, 1)
                    nc.vector.tensor_tensor(
                        high_hot[:, half, :, :], iota_n[:, :].unsqueeze(1).to_broadcast([P, 8, TILES]),
                        dst_high[:, bass.ds(first, 8)].unsqueeze(2).to_broadcast([P, 8, TILES]), ALU.is_equal).then_inc(hot, 1)
            dst_rows = edge_f[:, 0:2, :]
            nc.vector.tensor_reduce(tile_max[:, :], dst_rows, AX.X, ALU.max)
            step(nc.vector.tensor_scalar(no_pad[:, :, :], dst_rows, 0.0, BIG, ALU.is_lt, ALU.mult))
            step(nc.vector.tensor_tensor(no_pad[:, :, :], no_pad[:, :, :], dst_rows, ALU.add))
            step(nc.vector.tensor_reduce(tile_min[:, :], no_pad[:, :, :], AX.X, ALU.min))
            step(nc.vector.tensor_scalar(tile_min[:, :], tile_min[:, :], float(P), None, ALU.subtract))
            for g in range(2):
                nc.vector.tensor_scalar(candidates[:, g, :], tile_base[:, :], tile_max[:, g:g + 1],
                                        from_end[:, g:g + 1], ALU.is_le, ALU.mult).then_inc(cand, 1)
                nc.vector.tensor_scalar(candidates[:, 2 + g, :], tile_base[:, :], tile_min[:, g:g + 1],
                                        from_start[:, g:g + 1], ALU.is_gt, ALU.mult).then_inc(cand, 1)
            dve.wait_ge(maxed, 1)
            r = reduced[0:1, :, :]
            lo, hi, more = (window_f[:, k, :] for k in range(3))
            nc.vector.tensor_tensor(hi, r[:, 2, :], r[:, 3, :], ALU.max)
            step(nc.vector.tensor_tensor(lo, r[:, 0, :], r[:, 1, :], ALU.max))
            step(nc.vector.tensor_scalar(lo, lo, -1.0, 1000.0, ALU.mult, ALU.add))
            step(nc.vector.tensor_scalar(lo, lo, float(LAST_EDGE_TILE), None, ALU.min))
            step(nc.vector.tensor_tensor(more, hi, lo, ALU.subtract))
            step(nc.vector.tensor_scalar(more, more, float(WINDOW), 0.0, ALU.subtract, ALU.max))
            nc.vector.tensor_copy(t.first_edge_tile[:, :], lo).then_inc(tables, 1)
            nc.vector.tensor_copy(t.more_edge_tiles[:, :], more).then_inc(tables, 1)
            dve.wait_ge(counted, EDGE_TILES // 8 + 3)
            nc.vector.tensor_scalar(degree[:, :], degree_ps[:, :], 1.0, None, ALU.add).then_inc(tables, 1)
            dve.wait_ge(rooted, 1)
            nc.vector.memset(t.publish_scale[:, 2, :], 1.0)
            step(nc.vector.reciprocal(t.publish_scale[:, 0, :], degree[:, :]))
            step(nc.vector.tensor_copy(t.publish_scale[:, 1, :], t.publish_scale[:, 0, :]))
            nc.vector.tensor_scalar(t.node_base[:, :], tile_base[:, :], 0.0, None, ALU.add)
            nc.vector.memset(t.eps[:, :], EPS)
            dve.wait_ge(tables, 3)

        @block.scalar
        def _(act):
            act.wait_ge(tables, 3)
            nc.scalar.activation(degree[:, :], degree[:, :], ACT.Sqrt).then_inc(rooted, 1)

        @block.tensor
        def _(pe):
            pe.wait_ge(floats, 1)
            pe.wait_ge(consts, 10)
            for k in range(4):
                nc.tensor.transpose(turned[k][:, :], edge_f[:, k, :], t.ident[:, :]).then_inc(transposed, 1)
            nc.tensor.matmul(degree_ps[:, :], zeros[:, :], zeros[:, 0:TILES], start=True, stop=False)
            pe.sem_inc(counted, 2)
            with pe.Fori(0, EDGE_TILES // 16) as i:
                for half in range(2):
                    pe.wait_ge(hot, i * 4 + half * 2 + 2)
                    for k in range(8):
                        last = nc.tensor.matmul(degree_ps[:, :], low_hot[:, half, k, :], high_hot[:, half, k, :],
                                                start=False, stop=False)
                    last.then_inc(counted, 1)
            nc.tensor.matmul(degree_ps[:, :], zeros[:, :], zeros[:, 0:TILES], start=False, stop=True).then_inc(counted, 1)



def input_norm(nc, x, table, t):
    ctx = ExitStack()
    with ctx:
        def sb(name, shape, dt):
            return ctx.enter_context(nc.sbuf_tensor(name, shape, dt))

        def sem(name):
            return ctx.enter_context(nc.semaphore(name))

        RING = 4
        GROUPS = TILES // RING
        xin = sb("xin", [P, RING, D], FP32)
        out = sb("norm_out", [P, RING, D], FP32)
        stats = sb("norm_stats", [P, RING, 6], FP32)
        moments = sb("norm_moments", [P, RING, 2], FP32)
        std = sb("norm_std", [P, RING, 1], FP32)
        loaded = [sem(f"in_loaded{r}") for r in range(RING)]
        stored = [sem(f"in_stored{r}") for r in range(RING)]
        counted = sem("in_stats")
        averaged = sem("in_moments")
        rooted = sem("in_rooted")
        inverted = sem("in_inverted")
        normed = sem("in_normed")
        scaled = sem("in_scaled")
        passed = sem("in_passed")
        block = ctx.enter_context(nc.Block())

        @block.sync
        def _(sp):
            def load(n, r):
                sp.dma_start(xin[:, r, :], x[bass.ds(n * P, P), :]).then_inc(loaded[r], 16)

            def store(i, r):
                n = i * RING + r
                sp.wait_ge(scaled, n + 1)
                sp.dma_start(table[bass.ds(n * P, P), :], out[:, r, :]).then_inc(stored[r], 16)

            for r in range(RING):
                load(r, r)
                sp.sem_inc(stored[r], 16)
            with sp.Fori(0, GROUPS - 2) as i:
                for r in range(RING):
                    store(i, r)
                    sp.wait_ge(normed, i * RING + r + 1)
                    load((i + 1) * RING + r, r)
            for r in range(RING):
                n = (GROUPS - 1) * RING + r
                store(GROUPS - 2, r)
                sp.wait_ge(normed, (GROUPS - 2) * RING + r + 1)
                if n < FULL_TILES:
                    load(n, r)
                elif n == FULL_TILES:
                    sp.dma_start(xin[0:LAST_ROWS, r, :], x[FULL_TILES * P:NODES, :]).then_inc(loaded[r], 16)
                else:
                    sp.sem_inc(loaded[r], 16)
            for r in range(RING):
                store(GROUPS - 1, r)
            for r in range(RING):
                sp.wait_ge(stored[r], 16 * GROUPS + 16)

        @block.vector
        def _(dve):
            with dve.Fori(0, GROUPS) as i:
                for r in range(RING):
                    n = i * RING + r
                    dve.wait_ge(loaded[r], (i + 1) * 16)
                    nc.vector.bn_stats(stats[:, r, :], xin[:, r, :]).then_inc(counted, 1)
                    hold(dve, counted, n + 1, passed)
                    nc.vector.bn_aggr(moments[:, r, :], stats[:, r, :]).then_inc(averaged, 1)
                for r in range(RING):
                    n = i * RING + r
                    dve.wait_ge(rooted, n + 1)
                    nc.vector.reciprocal(std[:, r, :], std[:, r, :]).then_inc(inverted, 1)
                for r in range(RING):
                    n = i * RING + r
                    dve.wait_ge(inverted, n + 1)
                    nc.vector.tensor_scalar(t.rows[:, n, :], xin[:, r, :], moments[:, r, 0:1], std[:, r, :],
                                            ALU.subtract, ALU.mult).then_inc(normed, 1)

        @block.scalar
        def _(act):
            with act.Fori(0, GROUPS) as i:
                for r in range(RING):
                    n = i * RING + r
                    act.wait_ge(averaged, n + 1)
                    nc.scalar.activation(std[:, r, :], moments[:, r, 1:2], ACT.Sqrt, bias=t.eps[:, :]).then_inc(rooted, 1)
                for r in range(RING):
                    n = i * RING + r
                    act.wait_ge(stored[r], i * 16 + 16)
                    act.wait_ge(normed, n + 1)
                    nc.scalar.activation(out[:, r, :], t.rows[:, n, :], ACT.Copy,
                                         scale=t.publish_scale[:, 0, bass.ds(n, 1)]).then_inc(scaled, 1)


def beyond(nc, first, e):
    return nc.s_assert_within(first + e + WINDOW, min_val=WINDOW, max_val=EDGE_TILES - 1,
                              skip_runtime_bounds_check_because="more_edge_tiles counts up to LAST_EDGE_TILE")


def graph_layers(nc, table, W, b, gamma, beta, t):
    ctx = ExitStack()
    with ctx:
        def sb(name, shape, dt):
            return ctx.enter_context(nc.sbuf_tensor(name, shape, dt))

        def ps(name, shape, dt):
            return ctx.enter_context(nc.psum_tensor(name, shape, dt))

        def sem(name):
            return ctx.enter_context(nc.semaphore(name))

        PAIRS = TILES // 2
        STAGES = 4
        own = sb("own", [P, D], FP32)
        gathered = sb("gathered", [P, 2, WINDOW, D], FP32)
        extra = sb("extra", [P, D], FP32)
        sources = sb("sources", [P, 2, WINDOW], I32)
        extra_source = sb("extra_source", [P, 1], I32)
        dst_in_tile = sb("dst_in_tile", [P, 2, WINDOW], FP32)
        extra_dst = sb("extra_dst", [P, 1], FP32)
        choose = sb("choose", [P, 2, WINDOW, P], FP32)
        extra_choose = sb("extra_choose", [P, P], FP32)
        summed_high = sb("summed_high", [P, D], FP32R)
        summed_low = sb("summed_low", [P, D], FP32R)
        weights_high = sb("gnn_weights_high", [P, KT, D], FP32R)
        weights_low = sb("gnn_weights_low", [P, KT, D], FP32R)
        weight_rows = gathered[:, :, :, :].rearrange("p q s d -> p (q s) d")[:, 0:KT, :]
        stage = gathered[:, :, :, :].rearrange("p q s d -> p (q s) d")[:, 0:STAGES, :]
        square = gathered[:, :, :, :].rearrange("p q s d -> p (q s) d")[:, STAGES:STAGES + 2, :]
        bias = sb("gnn_bias", [P, D], FP32)
        total = sb("total", [P, D], FP32)
        mean = bias
        spare = choose[:, :, :, :].rearrange("p q s n -> p (q s n)")
        gamma_bc = spare[:, 0:D]
        ones = spare[:, D:D + P]
        beta_bc = extra

        sum_ps = [ps(f"sum_ps{q}", [P, D], FP32) for q in range(2)]
        z_ps = [ps(f"z_ps{q}", [P, D], FP32) for q in range(2)]
        turn_ps = [ps(f"turn_ps{q}", [P, D], FP32) for q in range(2)]
        mean_ps = ps("mean_ps", [P, D], FP32)
        square_ps = ps("square_ps", [P, D], FP32)

        table_stored = [sem(f"gl_table_stored{r}") for r in range(STAGES)]
        weights_loaded = sem("gl_weights_loaded")
        vectors_loaded = sem("gl_vectors_loaded")
        turned = sem("gl_weights_turned")
        high_ready = sem("gl_weights_high")
        low_ready = sem("gl_weights_low")
        source_ready = sem("gl_source_ready")
        fetched = [[sem(f"gl_fetched{q}{s}") for s in range(WINDOW)] for q in range(2)]
        own_ready = sem("gl_own_ready")
        choose_ready = sem("gl_choose_ready")
        sum_done = sem("gl_sum_done")
        sum_high = sem("gl_sum_high")
        sum_low = sem("gl_sum_low")
        z_done = sem("gl_z_done")
        z_read = sem("gl_z_read")
        total_done = sem("gl_total_done")
        x_source = sem("gl_extra_source")
        x_fetched = sem("gl_extra_fetched")
        x_dst = sem("gl_extra_dst")
        x_choose = sem("gl_extra_choose")
        x_used = sem("gl_extra_used")
        mean_done = sem("gl_mean_done")
        mean_ready = sem("gl_mean_ready")
        centred = sem("gl_centred")
        squared = sem("gl_squared")
        square_read = sem("gl_square_read")
        rooted = sem("gl_rooted")
        inverted = sem("gl_inverted")
        scale_ready = sem("gl_scale_ready")
        multiplied = sem("gl_multiplied")
        shifted = sem("gl_shifted")
        activated = sem("gl_activated")
        staged = sem("gl_staged")
        constant = sem("gl_ones")
        passed = sem("gl_passed")
        block = ctx.enter_context(nc.Block())

        @block.sync
        def _(sp):
            for r in range(STAGES):
                sp.sem_inc(table_stored[r], 16)
            sp.sem_inc(shifted, 1)
            with sp.Fori(0, LAYERS) as l:
                for r in range(STAGES):
                    sp.wait_ge(table_stored[r], l * (16 * TILES // STAGES) + 16)
                sp.dma_start(weight_rows[:, :, :],
                             W[bass.ds(l, 1), :, :].rearrange("l (k p) i -> p (l k) i", p=P)).then_inc(weights_loaded, 16)
                sp.wait_ge(shifted, l * TILES + 1)
                sp.dma_start(bias[:, :], b[bass.ds(l, 1), :].to_broadcast([P, D])).then_inc(vectors_loaded, 16)
                sp.wait_ge(sum_done, l * TILES + TILES + 2)
                for array, place in ((gamma, gamma_bc), (beta, beta_bc)):
                    sp.dma_start(place[:, :], array[bass.ds(l, 1), :].to_broadcast([P, D])).then_inc(vectors_loaded, 16)
                with sp.Fori(0, TILES // STAGES) as i:
                    for r in range(STAGES):
                        n = i * STAGES + r
                        sp.wait_ge(staged, l * TILES + n + 1)
                        sp.dma_start(table[bass.ds(n * P, P), :], stage[:, r, :]).then_inc(table_stored[r], 16)
            for r in range(STAGES):
                sp.wait_ge(table_stored[r], 16 * LAYERS * TILES // STAGES + 16)

        @block.gpsimd
        def _(pool):
            extras = pool.alloc_register("pool_extras")
            pool.reg_mov(extras, 0)
            with pool.Fori(0, LAYERS) as l:
                for r in range(STAGES):
                    pool.wait_ge(table_stored[r], l * (16 * TILES // STAGES) + 16)
                hold(pool, turned, l * KT + KT, passed)
                with pool.Fori(0, PAIRS) as i:
                    for q in range(2):
                        n = i * 2 + q
                        done = l * TILES + n
                        first = nc.gpsimd.value_load(t.first_edge_tile[0:1, bass.ds(n, 1)], min_val=0, max_val=LAST_EDGE_TILE)
                        pool.wait_ge(sum_done, done + 1)
                        nc.gpsimd.tensor_copy(sources[:, q, :], t.src_i[:, bass.ds(first, WINDOW)]).then_inc(source_ready, 1)
                        hold(pool, source_ready, done + 1, passed)
                        for s in range(WINDOW):
                            nc.gpsimd.indirect_dma_start(
                                out=gathered[:, q, s, :], out_offset=None, in_=table[:, :],
                                in_offset=bass.IndirectOffsetOnAxis(ap=sources[:, q, s:s + 1], axis=0),
                            ).then_inc(fetched[q][s], 16)
                        more = nc.gpsimd.value_load(t.more_edge_tiles[0:1, bass.ds(n, 1)], min_val=0, max_val=EDGE_TILES)
                        with pool.If(more > 0):
                            with pool.Fori(0, more) as e:
                                seen = pool.snap(extras)
                                pool.wait_ge(x_used, seen + 1)
                                nc.gpsimd.tensor_copy(extra_source[:, :],
                                                      t.src_i[:, bass.ds(beyond(nc, first, e), 1)]).then_inc(x_source, 1)
                                hold(pool, x_source, seen + 1, passed)
                                nc.gpsimd.indirect_dma_start(
                                    out=extra[:, :], out_offset=None, in_=table[:, :],
                                    in_offset=bass.IndirectOffsetOnAxis(ap=extra_source[:, 0:1], axis=0),
                                ).then_inc(x_fetched, 16)
                                pool.reg_add(extras, extras, 1)
                hold(pool, sum_done, l * TILES + TILES + 2, passed)
                nc.gpsimd.memset(ones[:, :], 1.0).then_inc(constant, 1)

        @block.vector
        def _(dve):
            extras = dve.alloc_register("dve_extras")
            dve.reg_mov(extras, 0)

            def build(l, n, q):
                done = l * TILES + n
                first = nc.vector.value_load(t.first_edge_tile[0:1, bass.ds(n, 1)], min_val=0, max_val=LAST_EDGE_TILE)
                more = nc.vector.value_load(t.more_edge_tiles[0:1, bass.ds(n, 1)], min_val=0, max_val=EDGE_TILES)
                dve.wait_ge(sum_done, done + 1)
                nc.vector.tensor_scalar(dst_in_tile[:, q, :], t.dst_f[:, bass.ds(first, WINDOW)],
                                        t.node_base[:, bass.ds(n, 1)], None, ALU.subtract).then_inc(choose_ready, 1)
                dve.wait_ge(choose_ready, done * 2 + 1)
                nc.vector.tensor_tensor(choose[:, q, :, :], t.iota[:, :].unsqueeze(1).to_broadcast([P, WINDOW, P]),
                                        dst_in_tile[:, q, :].unsqueeze(2).to_broadcast([P, WINDOW, P]),
                                        ALU.is_equal).then_inc(choose_ready, 1)
                with dve.If(more > 0):
                    with dve.Fori(0, more) as e:
                        seen = dve.snap(extras)
                        dve.wait_ge(x_used, seen + 1)
                        nc.vector.tensor_scalar(extra_dst[:, :], t.dst_f[:, bass.ds(beyond(nc, first, e), 1)],
                                                t.node_base[:, bass.ds(n, 1)], None, ALU.subtract).then_inc(x_dst, 1)
                        dve.wait_ge(x_dst, seen + 1)
                        nc.vector.tensor_scalar(extra_choose[:, :], t.iota[:, :], extra_dst[:, 0:1], None,
                                                ALU.is_equal).then_inc(x_choose, 1)
                        dve.reg_add(extras, extras, 1)

            def lower_sum(l, n, q):
                dve.wait_ge(sum_high, l * TILES + n + 1)
                nc.vector.tensor_tensor(summed_low[:, :], sum_ps[q][:, :], summed_high[:, :].bitcast(FP32),
                                        ALU.subtract).then_inc(sum_low, 1)

            def finish(l, n, q, mask=None):
                done = l * TILES + n
                dve.wait_ge(z_done, done + 3)
                nc.vector.scalar_tensor_tensor(t.rows[:, n, :], z_ps[q][:, :], t.publish_scale[:, 0, bass.ds(n, 1)],
                                               bias[:, :], ALU.mult, ALU.add).then_inc(z_read, 1)
                dve.wait_ge(total_done, done + l + 1)
                dve.wait_ge(z_read, done + 3)
                if mask is None:
                    nc.vector.tensor_tensor(total[:, :], t.rows[:, n, :], total[:, :], ALU.add
                                            ).then_inc(total_done, 1)
                else:
                    nc.vector.scalar_tensor_tensor(total[:, :], t.rows[:, n, :], mask, total[:, :], ALU.mult,
                                                   ALU.add).then_inc(total_done, 1)

            for q in range(2):
                dve.sem_inc(z_read, 1)
                dve.sem_inc(sum_low, 1)
            with dve.Fori(0, LAYERS) as l:
                dve.wait_ge(vectors_loaded, l * 48 + 16)
                dve.wait_ge(mean_done, l + 1)
                nc.vector.memset(total[:, :], 0.0).then_inc(total_done, 1)
                for k in range(KT):
                    dve.wait_ge(high_ready, l * KT + k + 1)
                    nc.vector.tensor_tensor(weights_low[:, k, :], turn_ps[k % 2][:, :],
                                            weights_high[:, k, :].bitcast(FP32), ALU.subtract).then_inc(low_ready, 1)
                build(l, 0, 0)
                build(l, 1, 1)
                with dve.Fori(0, PAIRS - 1) as i:
                    for q in range(2):
                        lower_sum(l, i * 2 + q, q)
                        build(l, i * 2 + q + 2, q)
                        finish(l, i * 2 + q, q)
                for q in range(2):
                    lower_sum(l, TILES - 2 + q, q)
                    finish(l, TILES - 2 + q, q, t.mask[:, q:q + 1])
                dve.wait_ge(mean_done, l + 2)
                dve.wait_ge(z_read, l * TILES + TILES + 2)
                nc.vector.tensor_scalar(mean[:, :], mean_ps[:, :], 1.0 / NODES, None, ALU.mult).then_inc(mean_ready, 1)
                hold(dve, mean_ready, l + 1, passed)
                with dve.Fori(0, PAIRS) as i:
                    for q in range(2):
                        n = i * 2 + q
                        nc.vector.tensor_tensor(t.rows[:, n, :], t.rows[:, n, :], mean[:, :],
                                                ALU.subtract).then_inc(centred, 1)
                dve.wait_ge(rooted, l + 1)
                nc.vector.reciprocal(total[:, :], total[:, :]).then_inc(inverted, 1)
                dve.wait_ge(inverted, l + 1)
                dve.wait_ge(vectors_loaded, l * 48 + 48)
                nc.vector.tensor_tensor(gamma_bc[:, :], gamma_bc[:, :], total[:, :], ALU.mult).then_inc(scale_ready, 1)
                hold(dve, scale_ready, l + 1, passed)
                with dve.Fori(0, PAIRS) as i:
                    first = i * 2
                    done = l * TILES + first
                    for q in range(2):
                        nc.vector.tensor_tensor(t.rows[:, first + q, :], t.rows[:, first + q, :], gamma_bc[:, :],
                                                ALU.mult).then_inc(multiplied, 1)
                    for q in range(2):
                        dve.wait_ge(multiplied, done + q + 1)
                        nc.vector.tensor_tensor(t.rows[:, first + q, :], t.rows[:, first + q, :], beta_bc[:, :],
                                                ALU.add).then_inc(shifted, 1)

        @block.scalar
        def _(act):
            def scale_own(l, n, q):
                done = l * TILES + n
                act.wait_ge(sum_done, done + 2)
                nc.scalar.activation(own[:, :], t.rows[:, n, :], ACT.Copy,
                                     scale=t.publish_scale[:, 0, bass.ds(n, 1)]).then_inc(own_ready, 1)

            def copy_sum(l, n, q):
                done = l * TILES + n
                act.wait_ge(sum_done, done + 3)
                act.wait_ge(z_done, done + 2)
                nc.scalar.activation(summed_high[:, :], sum_ps[q][:, :], ACT.Copy).then_inc(sum_high, 1)

            act.sem_inc(activated, 1)
            with act.Fori(0, LAYERS) as l:
                act.wait_ge(activated, l * TILES + 1)
                for k in range(KT):
                    act.wait_ge(turned, l * KT + k + 1)
                    nc.scalar.activation(weights_high[:, k, :], turn_ps[k % 2][:, :], ACT.Copy).then_inc(high_ready, 1)
                scale_own(l, 0, 0)
                with act.Fori(0, PAIRS - 1) as i:
                    scale_own(l, i * 2 + 1, 1)
                    copy_sum(l, i * 2, 0)
                    scale_own(l, i * 2 + 2, 0)
                    copy_sum(l, i * 2 + 1, 1)
                scale_own(l, TILES - 1, 1)
                copy_sum(l, TILES - 2, 0)
                copy_sum(l, TILES - 1, 1)
                hold(act, z_done, l * TILES + TILES + 2, passed)

                def squares(n, q, mask=1.0):
                    done = l * TILES + n
                    act.wait_ge(centred, done + 1)
                    act.wait_ge(square_read, done + 1)
                    nc.scalar.activation(square[:, q, :], t.rows[:, n, :], ACT.Square, scale=mask
                                         ).then_inc(squared, 1)

                with act.Fori(0, PAIRS - 1) as i:
                    for q in range(2):
                        squares(i * 2 + q, q)
                for q in range(2):
                    squares(TILES - 2 + q, q, t.mask[:, q:q + 1])
                act.wait_ge(square_read, l * TILES + TILES + 2)
                nc.scalar.activation(total[:, :], square_ps[:, :], ACT.Sqrt, bias=t.eps[:, :],
                                     scale=1.0 / NODES).then_inc(rooted, 1)
                with act.Fori(0, TILES // STAGES) as i:
                    for r in range(STAGES):
                        n = i * STAGES + r
                        act.wait_ge(shifted, l * TILES + n + 2)
                        nc.scalar.activation(t.rows[:, n, :], t.rows[:, n, :], ACT.Relu).then_inc(activated, 1)
                    for r in range(STAGES):
                        n = i * STAGES + r
                        act.wait_ge(activated, l * TILES + n + 2)
                        act.wait_ge(table_stored[r], l * (16 * TILES // STAGES) + i * 16 + 16)
                        nc.scalar.activation(stage[:, r, :], t.rows[:, n, :], ACT.Copy,
                                             scale=t.publish_scale[:, bass.ds(l + 0, 1), bass.ds(n, 1)]
                                             .rearrange("p a b -> p (a b)")).then_inc(staged, 1)

        @block.tensor
        def _(pe):
            extras = pe.alloc_register("pe_extras")
            pe.reg_mov(extras, 0)

            def sum_edges(l, i, q, n):
                done = l * TILES + n
                more = nc.tensor.value_load(t.more_edge_tiles[0:1, bass.ds(n, 1)], min_val=0, max_val=EDGE_TILES)
                pe.wait_ge(sum_low, done + 1)
                pe.wait_ge(choose_ready, done * 2 + 2)
                for s in range(WINDOW):
                    pe.wait_ge(fetched[q][s], (l * PAIRS + i) * 16 + 16)
                    for k in range(KT):
                        nc.tensor.matmul(sum_ps[q][:, k * P:(k + 1) * P], gathered[:, q, s, k * P:(k + 1) * P],
                                         choose[:, q, s, :], start=(s == 0 and k == 0), stop=False,
                                         skip_group_check=True)
                with pe.If(more > 0):
                    with pe.Fori(0, more):
                        seen = pe.snap(extras)
                        pe.wait_ge(x_choose, seen + 1)
                        pe.wait_ge(x_fetched, seen * 16 + 16)
                        for k in range(KT):
                            last = nc.tensor.matmul(sum_ps[q][:, k * P:(k + 1) * P], extra[:, k * P:(k + 1) * P],
                                                    extra_choose[:, :], start=False, stop=False,
                                                    skip_group_check=True)
                        last.then_inc(x_used, 1)
                        pe.reg_add(extras, extras, 1)
                pe.wait_ge(own_ready, done + 1)
                for k in range(KT):
                    last = nc.tensor.matmul(sum_ps[q][:, k * P:(k + 1) * P], own[:, k * P:(k + 1) * P],
                                            t.ident[:, :], start=False, stop=True, skip_group_check=True)
                last.then_inc(sum_done, 1)

            def product(l, n, q):
                done = l * TILES + n
                pe.wait_ge(z_read, done + 1)
                pe.wait_ge(sum_low, done + 3)
                parts = ((summed_high, weights_high), (summed_high, weights_low), (summed_low, weights_high))
                for k in range(KT):
                    for part, (summed, weights) in enumerate(parts):
                        last = nc.tensor.matmul(z_ps[q][:, :], summed[:, k * P:(k + 1) * P], weights[:, k, :],
                                                start=(k == 0 and part == 0), stop=(k == KT - 1 and part == 2))
                last.then_inc(z_done, 1)

            pe.sem_inc(mean_done, 1)
            pe.sem_inc(x_used, 1)
            for q in range(2):
                pe.sem_inc(sum_done, 1)
                pe.sem_inc(z_done, 1)
                pe.sem_inc(square_read, 1)
            with pe.Fori(0, LAYERS) as l:
                pe.wait_ge(weights_loaded, l * 16 + 16)
                for k in range(KT):
                    if k >= 2:
                        pe.wait_ge(low_ready, l * KT + k - 1)
                    for o in range(KT):
                        last = nc.tensor.transpose(turn_ps[k % 2][:, o * P:(o + 1) * P],
                                                   weight_rows[:, o, k * P:(k + 1) * P], t.ident[:, :])
                    last.then_inc(turned, 1)
                hold(pe, low_ready, l * KT + KT, passed)
                sum_edges(l, 0, 0, 0)
                with pe.Fori(0, PAIRS - 1) as i:
                    sum_edges(l, i, 1, i * 2 + 1)
                    product(l, i * 2, 0)
                    sum_edges(l, i + 1, 0, i * 2 + 2)
                    product(l, i * 2 + 1, 1)
                sum_edges(l, PAIRS - 1, 1, TILES - 1)
                product(l, TILES - 2, 0)
                product(l, TILES - 1, 1)
                pe.wait_ge(constant, l + 1)
                pe.wait_ge(total_done, l * (TILES + 1) + TILES + 1)
                nc.tensor.matmul(mean_ps[:, :], ones[:, :], total[:, :], start=True, stop=True).then_inc(mean_done, 1)

                def add_square(i, q, start, stop):
                    pe.wait_ge(squared, l * TILES + i * 2 + q + 1)
                    return nc.tensor.matmul(square_ps[:, :], ones[:, :], square[:, q, :], start=start,
                                            stop=stop).then_inc(square_read, 1)

                add_square(0, 0, True, False)
                add_square(0, 1, False, False)
                with pe.Fori(1, PAIRS - 1) as i:
                    add_square(i, 0, False, False)
                    add_square(i, 1, False, False)
                add_square(PAIRS - 1, 0, False, False)
                add_square(PAIRS - 1, 1, False, True)


def gate_inputs(nc, x, table, residual, gate_in, w_gates, b_gates, w_state, t):
    ctx = ExitStack()
    with ctx:
        def sb(name, shape, dt):
            return ctx.enter_context(nc.sbuf_tensor(name, shape, dt))

        def ps(name, shape, dt):
            return ctx.enter_context(nc.psum_tensor(name, shape, dt))

        def sem(name):
            return ctx.enter_context(nc.semaphore(name))

        G = GATES * D
        weights = sb("input_weights", [P, KT, KT, GATES, P], FP32)
        weights_high = sb("input_weights_high", [P, KT, KT, GATES, P], FP32R)
        weights_low = sb("input_weights_low", [P, KT, KT, GATES, P], FP32R)
        bias = sb("gate_bias", [P, KT, GATES, P], FP32)
        xin = sb("gi_x", [P, 2, D], FP32)
        gnn = sb("gi_gnn", [P, 2, D], FP32)
        res = sb("gi_res", [P, 2, D], FP32)
        normed = sb("gi_normed", [P, 2, D], FP32)
        high = sb("gi_high", [P, 2, D], FP32R)
        low = sb("gi_low", [P, 2, D], FP32R)
        out = sb("gi_out", [P, 2, G], FP32)
        stats = sb("gi_stats", [P, 2, 6], FP32)
        moments = sb("gi_moments", [P, 2, 2], FP32)
        std = sb("gi_std", [P, 2, 1], FP32)
        gate_ps = [ps(f"gate_ps{j}", [P, D], FP32) for j in range(KT)]
        turn_ps = ps("gi_turn_ps", [P, D], FP32)

        weights_loaded = sem("gi_weights_loaded")
        x_loaded = [sem(f"gi_x_loaded{q}") for q in range(2)]
        gnn_loaded = [sem(f"gi_gnn_loaded{q}") for q in range(2)]
        res_stored = [sem(f"gi_res_stored{q}") for q in range(2)]
        out_stored = [sem(f"gi_out_stored{q}") for q in range(2)]
        out_free = [sem(f"gi_out_free{q}") for q in range(2)]
        res_ready = sem("gi_res_ready")
        passed = sem("gi_passed")
        averaged = sem("gi_averaged")
        rooted = sem("gi_rooted")
        inverted = sem("gi_inverted")
        norm_ready = sem("gi_norm_ready")
        turn_done = sem("gi_turn_done")
        high_ready = sem("gi_high_ready")
        low_ready = sem("gi_low_ready")
        weights_split = sem("gi_weights_split")
        gate_done = [sem(f"gi_gate_done{j}") for j in range(KT)]
        gate_read = [sem(f"gi_gate_read{j}") for j in range(KT)]
        block = ctx.enter_context(nc.Block())
        PAIRS = TILES // 2

        @block.sync
        def _(sp):
            def load(n, q):
                sp.dma_start(gnn[:, q, :], table[bass.ds(n * P, P), :]).then_inc(gnn_loaded[q], 16)
                sp.dma_start(xin[:, q, :], x[bass.ds(n * P, P), :]).then_inc(x_loaded[q], 16)

            def store(n, q):
                sp.wait_ge(res_ready, n + 1)
                sp.dma_start(residual[bass.ds(n * P, P), :], res[:, q, :]).then_inc(res_stored[q], 16)

            load(0, 0)
            load(1, 1)
            for q in range(2):
                sp.sem_inc(res_stored[q], 16)
            for g in range(GATES):
                for k in range(KT):
                    sp.dma_start(weights[:, k, :, g, :],
                                 w_gates[g][k * P:(k + 1) * P, :].rearrange("p (j u) -> p j u", u=P)
                                 ).then_inc(weights_loaded, 16)
                sp.dma_start(bias[:, :, g, :], b_gates[g].rearrange("(j u) -> j u", u=P).partition_broadcast(P)
                             ).then_inc(weights_loaded, 16)
            with sp.Fori(0, PAIRS - 2) as i:
                for q in range(2):
                    store(i * 2 + q, q)
                    load(i * 2 + q + 2, q)
            for g in range(GATES):
                for k in range(KT):
                    sp.dma_start(t.state_weights[:, k, :, g, :],
                                 w_state[g][k * P:(k + 1) * P, :].rearrange("p (j u) -> p j u", u=P)
                                 ).then_inc(t.state_loaded, 16)
            for q in range(2):
                n = FULL_TILES + q
                store(n - 2, q)
                sp.dma_start(gnn[:, q, :], table[n * P:(n + 1) * P, :]).then_inc(gnn_loaded[q], 16)
                if q == 0:
                    sp.dma_start(xin[0:LAST_ROWS, q, :], x[n * P:NODES, :]).then_inc(x_loaded[q], 16)
                else:
                    sp.sem_inc(x_loaded[q], 16)
            for q in range(2):
                store(FULL_TILES + q, q)
            for q in range(2):
                sp.wait_ge(res_stored[q], 16 * PAIRS + 16)

        @block.gpsimd
        def _(pool):
            with pool.Fori(0, PAIRS) as i:
                for q in range(2):
                    pool.wait_ge(gate_read[KT - 1], i * 2 + q + 2)
                    pool.dma_start(gate_in[bass.ds((i * 2 + q) * P, P), :], out[:, q, :]).then_inc(out_stored[q], 16)
                    pool.wait_ge(out_stored[q], i * 16 + 16)
                    pool.sem_inc(out_free[q], 1)

        @block.vector
        def _(dve):
            def norm(i, n, q):
                dve.wait_ge(x_loaded[q], i * 16 + 16)
                dve.wait_ge(gnn_loaded[q], i * 16 + 16)
                dve.wait_ge(res_stored[q], i * 16 + 16)
                nc.vector.tensor_tensor(res[:, q, :], xin[:, q, :], gnn[:, q, :], ALU.add).then_inc(res_ready, 1)
                dve.wait_ge(res_ready, n + 1)
                nc.vector.bn_stats(stats[:, q, :], res[:, q, :]).then_inc(averaged, 1)
                hold(dve, averaged, n * 2 + 1, passed)
                nc.vector.bn_aggr(moments[:, q, :], stats[:, q, :]).then_inc(averaged, 1)
                dve.wait_ge(rooted, n + 1)
                nc.vector.reciprocal(std[:, q, :], std[:, q, :]).then_inc(inverted, 1)
                dve.wait_ge(inverted, n + 1)
                nc.vector.tensor_scalar(normed[:, q, :], res[:, q, :], moments[:, q, 0:1], std[:, q, :],
                                        ALU.subtract, ALU.mult).then_inc(norm_ready, 1)

            def lower(n, q):
                dve.wait_ge(high_ready, n + 1)
                nc.vector.tensor_tensor(low[:, q, :], turn_ps[:, :], high[:, q, :].bitcast(FP32), ALU.subtract
                                        ).then_inc(low_ready, 1)

            def add_bias(i, n, q, unit_tiles):
                dve.wait_ge(out_free[q], i + 1)
                for j in unit_tiles:
                    dve.wait_ge(gate_done[j], n + 1)
                    nc.vector.tensor_tensor(out[:, q, j * D:(j + 1) * D], gate_ps[j][:, :],
                                            bias[:, j, :, :].rearrange("p g u -> p (g u)"),
                                            ALU.add).then_inc(gate_read[j], 1)

            dve.sem_inc(low_ready, 1)
            for j in range(KT):
                dve.sem_inc(gate_read[j], 1)
            for q in range(2):
                dve.sem_inc(out_free[q], 1)
            norm(0, 0, 0)
            lower(0, 0)
            dve.wait_ge(weights_loaded, 16 * GATES * (KT + 1))
            for k in range(KT):
                nc.vector.tensor_copy(weights_high[:, k, :, :, :], weights[:, k, :, :, :]).then_inc(weights_split, 1)
            for k in range(KT):
                dve.wait_ge(weights_split, k + 1)
                nc.vector.tensor_tensor(weights_low[:, k, :, :, :], weights[:, k, :, :, :],
                                        weights_high[:, k, :, :, :].bitcast(FP32), ALU.subtract
                                        ).then_inc(weights_split, 1)
            with dve.Fori(0, PAIRS - 1) as i:
                norm(i, i * 2 + 1, 1)
                add_bias(i, i * 2, 0, range(0, 2))
                lower(i * 2 + 1, 1)
                add_bias(i, i * 2, 0, range(2, KT))
                norm(i + 1, i * 2 + 2, 0)
                add_bias(i, i * 2 + 1, 1, range(0, 2))
                lower(i * 2 + 2, 0)
                add_bias(i, i * 2 + 1, 1, range(2, KT))
            norm(PAIRS - 1, TILES - 1, 1)
            add_bias(PAIRS - 1, TILES - 2, 0, range(0, 2))
            lower(TILES - 1, 1)
            add_bias(PAIRS - 1, TILES - 2, 0, range(2, KT))
            add_bias(PAIRS - 1, TILES - 1, 1, range(KT))

        @block.scalar
        def _(act):
            def serve(n, q):
                act.wait_ge(averaged, n * 2 + 2)
                nc.scalar.activation(std[:, q, :], moments[:, q, 1:2], ACT.Sqrt, bias=t.eps[:, :]).then_inc(rooted, 1)
                act.wait_ge(turn_done, n + 1)
                nc.scalar.activation(high[:, q, :], turn_ps[:, :], ACT.Copy).then_inc(high_ready, 1)

            with act.Fori(0, PAIRS) as i:
                for q in range(2):
                    serve(i * 2 + q, q)

        @block.tensor
        def _(pe):
            def turn(n, q):
                pe.wait_ge(norm_ready, n + 1)
                pe.wait_ge(low_ready, n + 1)
                for k in range(KT):
                    last = nc.tensor.transpose(turn_ps[:, k * P:(k + 1) * P], normed[:, q, k * P:(k + 1) * P],
                                               t.ident[:, :])
                last.then_inc(turn_done, 1)

            def product(n, q, j):
                pe.wait_ge(gate_read[j], n + 1)
                parts = ((high, weights_high), (high, weights_low), (low, weights_high))
                for k in range(KT):
                    for part, (turned, weight) in enumerate(parts):
                        last = nc.tensor.matmul(gate_ps[j][:, :], turned[:, q, k * P:(k + 1) * P],
                                                weight[:, k, j, :, :].rearrange("p g u -> p (g u)"),
                                                start=(k == 0 and part == 0), stop=(k == KT - 1 and part == 2))
                last.then_inc(gate_done[j], 1)

            def tile(n, q, more=True):
                pe.wait_ge(low_ready, n + 2)
                product(n, q, 0)
                product(n, q, 1)
                if more:
                    turn(n + 1, 1 - q)
                product(n, q, 2)
                product(n, q, 3)

            turn(0, 0)
            pe.wait_ge(weights_split, 2 * KT)
            with pe.Fori(0, PAIRS - 1) as i:
                tile(i * 2, 0)
                tile(i * 2 + 1, 1)
            tile(TILES - 2, 0)
            tile(TILES - 1, 1, more=False)


def recurrence(nc, residual, gate_in, out, t):
    ctx = ExitStack()
    with ctx:
        def sb(name, shape, dt):
            return ctx.enter_context(nc.sbuf_tensor(name, shape, dt))

        def ps(name, shape, dt):
            return ctx.enter_context(nc.psum_tensor(name, shape, dt))

        def sem(name):
            return ctx.enter_context(nc.semaphore(name))

        STEPS = ROWS // P
        CHAINS = NODES // STEPS
        BLOCK = 10
        BLOCKS = STEPS // BLOCK
        CHECK_AT = 5
        GROUP = 5
        TOLERANCE = 2.0 ** -18
        G = GATES * D
        C, H = 0, 1
        STORE_SPLIT = CHAINS // 16 * 16

        weights_high = sb("state_weights_high", [P, KT, KT, GATES, P], FP32R)
        weights_low = sb("state_weights_low", [P, KT, KT, GATES, P], FP32R)
        inputs = sb("inputs", [P, 2, G], FP32)
        res = sb("res", [P, 2, D], FP32)
        result = sb("result", [P, 2, D], FP32)
        before = sb("before", [P, KT, GATES, P], FP32)
        gates = sb("gates", [P, KT, GATES, P], FP32)
        state = sb("state", [P, 2, D], FP32)
        kept = sb("kept", [P, KT, P], FP32)
        added = sb("added", [P, KT, P], FP32)
        squashed = sb("squashed", [P, KT, P], FP32)
        h_high = sb("h_high", [P, KT, P], FP32R)
        h_low = sb("h_low", [P, KT, P], FP32R)
        shift = sb("shift", [P, P], FP32)
        snap = sb("snap", [P, 2, D], FP32)
        history = sb("history", [P, BLOCKS, 2, D], FP32)
        change = sb("change", [P, 2, D], FP32)
        allowed = sb("allowed", [P, 2, D], FP32)
        excess = sb("excess", [P, 2, D], FP32)
        worst = sb("worst", [P, 1], FP32)
        worst_all = sb("worst_all", [P, 1], FP32)
        go_on = sb("go_on", [P, 1], I32)
        gate_ps = [ps(f"cell_ps{j}", [P, D], FP32) for j in range(KT)]
        turn_ps = [ps(f"cell_turn_ps{j}", [P, P], FP32) for j in range(KT)]

        weights_split = sem("re_weights_split")
        inputs_loaded = [sem(f"re_inputs_loaded{q}") for q in range(2)]
        res_loaded = [sem(f"re_res_loaded{q}") for q in range(2)]
        stored = [sem(f"re_stored{q}") for q in range(2)]
        shift_ready = sem("re_shift_ready")
        history_ready = sem("re_history_ready")
        gate_done = [sem(f"re_gate_done{j}") for j in range(KT)]
        gate_read = [sem(f"re_gate_read{j}") for j in range(KT)]
        gates_ready = [sem(f"re_gates_ready{j}") for j in range(KT)]
        product_ready = sem("re_product_ready")
        c_ready = [sem(f"re_c_ready{j}") for j in range(KT)]
        squash_ready = [sem(f"re_squash_ready{j}") for j in range(KT)]
        h_ready = [sem(f"re_h_ready{j}") for j in range(KT)]
        turned = [sem(f"re_turned{j}") for j in range(KT)]
        high_ready = [sem(f"re_high_ready{j}") for j in range(KT)]
        low_ready = [sem(f"re_low_ready{j}") for j in range(KT)]
        moved = sem("re_moved")
        c_moved = sem("re_c_moved")
        result_ready = sem("re_result_ready")
        snapped = sem("re_snapped")
        check = sem("re_check")
        excess_ready = sem("re_excess_ready")
        worst_ready = sem("re_worst_ready")
        flag_ready = sem("re_flag_ready")
        flag_seen = sem("re_flag_seen")
        passed = sem("re_passed")
        block_ = ctx.enter_context(nc.Block())

        by_step_in = gate_in.rearrange("(c t) f -> t c f", t=STEPS)
        by_step_res = residual.rearrange("(c t) f -> t c f", t=STEPS)
        by_step_out = out.rearrange("(c t) f -> t c f", t=STEPS)

        def uses(done, pair):
            return done * (BLOCK // 2) + pair

        def sweeps(eng, begin, step, prologue=None):
            go = eng.alloc_register("go")
            eng.reg_mov(go, 1)
            def one_sweep(sweep):
                with eng.If(eng.snap(go) > 0):
                    if begin:
                        begin(sweep, sweep * STEPS)
                    with eng.Fori(0, BLOCKS) as b:
                        with eng.If(eng.snap(go) > 0):
                            done = sweep * BLOCKS + b
                            if prologue:
                                prologue(done * BLOCK)
                            for k in range(BLOCK):
                                step(sweep, done, b, k // 2, k, k % 2)
                            hold(eng, flag_ready, done + 1, passed)
                            eng.reg_load(go, go_on[0:1, 0:1]).then_inc(flag_seen, 1)
                        eng.sem_inc(passed, 1)
                eng.sem_inc(passed, 1)

            with eng.Fori(0, CHAINS // GROUP) as group:
                with eng.If(eng.snap(go) > 0):
                    with eng.Fori(0, GROUP) as s:
                        one_sweep(group * GROUP + s)
                eng.sem_inc(passed, 1)

        @block_.sync
        def _(sp):
            def load_inputs(tile, q):
                sp.dma_start(inputs[:, q, :], by_step_in[bass.ds(tile, 1), :, :].rearrange("t c f -> c (t f)")
                             ).then_inc(inputs_loaded[q], 16)

            def load_res(tile, q):
                sp.dma_start(res[:, q, :], by_step_res[bass.ds(tile, 1), :, :].rearrange("t c f -> c (t f)")
                             ).then_inc(res_loaded[q], 16)

            def step(sweep, done, b, pair, k, q):
                count = done * BLOCK + k
                ahead = (b * BLOCK + k + 2) % STEPS
                sp.wait_ge(gate_read[KT - 1], count + 2)
                load_inputs(ahead, q)
                sp.wait_ge(result_ready, count + 2)
                tile = b * BLOCK + k
                for a, z in ((0, STORE_SPLIT), (STORE_SPLIT, CHAINS)):
                    sp.dma_start(by_step_out[bass.ds(tile, 1), a:z, :].rearrange("t c f -> c (t f)"),
                                 result[a:z, q, :]).then_inc(stored[q], 16)
                load_res(ahead, q)

            for q in range(2):
                load_inputs(q, q)
                load_res(q, q)
                sp.sem_inc(stored[q], 32)
            blocks = sp.alloc_register("blocks_run")
            sp.reg_mov(blocks, 0)

            def counted_step(sweep, done, b, pair, k, q):
                step(sweep, done, b, pair, k, q)
                if k == BLOCK - 1:
                    sp.reg_add(blocks, blocks, 1)

            sweeps(sp, None, counted_step)
            ran = sp.snap(blocks)
            for q in range(2):
                hold(sp, stored[q], ran * (BLOCK * 16) + 32, passed)
                hold(sp, inputs_loaded[q], ran * (BLOCK * 8) + 16, passed)
                hold(sp, res_loaded[q], ran * (BLOCK * 8) + 16, passed)

        @block_.gpsimd
        def _(pool):
            nc.gpsimd.memset(shift[:, :], 0.0).then_inc(shift_ready, 1)
            pool.wait_ge(shift_ready, 1)
            nc.gpsimd.affine_select(out=shift[:, :], in_=shift[:, :], compare_op=ALU.not_equal, fill=1.0, base=1,
                                    pattern=[[-1, P]], channel_multiplier=1).then_inc(shift_ready, 1)
            nc.gpsimd.memset(history[:, :, :, :], 1e15).then_inc(history_ready, 1)
            nc.gpsimd.memset(excess[:, :, :], -1.0).then_inc(history_ready, 1)
            pool.wait_ge(history_ready, 2)

            def step(sweep, done, b, pair, k, q):
                count = done * BLOCK + k
                pool.wait_ge(res_loaded[q], uses(done, pair) * 16 + 16)
                pool.wait_ge(stored[q], uses(done, pair) * 32 + 32)
                hold(pool, h_ready[KT - 1], count + sweep + 3, passed)
                nc.gpsimd.tensor_tensor(result[:, q, :], state[:, H, :], res[:, q, :], ALU.add
                                        ).then_inc(result_ready, 1)
                rows = slice(0, CHAINS)
                old = history[rows, bass.ds(b, 1), :, :].rearrange("p b s d -> p (b s) d")
                if k == CHECK_AT:
                    pool.wait_ge(snapped, done + 1)
                    nc.gpsimd.tensor_tensor(change[rows], snap[rows], old, ALU.subtract)
                    nc.gpsimd.tensor_tensor(allowed[rows], snap[rows], snap[rows], ALU.mult).then_inc(check, 1)
                if k == CHECK_AT + 1:
                    pool.wait_ge(check, done * 5 + 2)
                    nc.gpsimd.tensor_tensor(change[rows], change[rows], change[rows], ALU.mult)
                    nc.gpsimd.tensor_scalar(allowed[rows], allowed[rows], 1.0, TOLERANCE * TOLERANCE, ALU.max,
                                            ALU.mult).then_inc(check, 1)
                if k == CHECK_AT + 2:
                    pool.wait_ge(check, done * 5 + 3)
                    nc.gpsimd.tensor_tensor(excess[rows], change[rows], allowed[rows], ALU.subtract
                                            ).then_inc(excess_ready, 1)
                    nc.gpsimd.tensor_copy(old, snap[rows]).then_inc(check, 2)
                if k == CHECK_AT + 3:
                    hold(pool, worst_ready, done + 1, passed)
                    nc.gpsimd.partition_all_reduce(worst_all[:, :], worst[:, :], P,
                                                   bass.bass_isa.ReduceOp.max).then_inc(check, 1)
                    pool.wait_ge(check, done * 5 + 6)
                    hold(pool, flag_seen, done * 5 + 1, passed)
                    nc.gpsimd.tensor_scalar(go_on[:, :], worst_all[:, :], 0.0, None, ALU.is_gt).then_inc(flag_ready, 1)

            pool.sem_inc(result_ready, 1)
            pool.sem_inc(flag_seen, 1)
            pool.sem_inc(check, 1)
            sweeps(pool, None, step)

        @block_.vector
        def _(dve):
            nc.vector.memset(state[:, C, :], 0.0)
            for j in range(KT):
                nc.vector.memset(state[:, H, j * P:(j + 1) * P], 0.0).then_inc(h_ready[j], 1)
            for j in range(KT):
                dve.sem_inc(gate_read[j], 1)

            def lower(j, value):
                dve.wait_ge(high_ready[j], value)
                nc.vector.tensor_tensor(h_low[:, j, :], turn_ps[j][:, :], h_high[:, j, :].bitcast(FP32),
                                        ALU.subtract).then_inc(low_ready[j], 1)
            
            def begin(sweep, steps):
                dve.wait_ge(moved, sweep * 2 + 1)
                nc.vector.tensor_copy(state[:, C, :], gate_ps[0][:, :]).then_inc(c_moved, 1)
                dve.wait_ge(moved, sweep * 2 + 2)
                dve.wait_ge(result_ready, steps + 1)
                for j in range(KT):
                    nc.vector.tensor_copy(state[:, H, j * P:(j + 1) * P],
                                          gate_ps[1][:, j * P:(j + 1) * P]).then_inc(h_ready[j], 1)
                hold(dve, c_moved, sweep + 1, passed)
                lower(0, steps + sweep + 1)

            def step(sweep, done, b, pair, k, q):
                count = done * BLOCK + k
                last = k == BLOCK - 1

                def add(j):
                    if j == 0:
                        dve.wait_ge(inputs_loaded[q], uses(done, pair) * 16 + 16)
                    dve.wait_ge(gate_done[j], count + 1)
                    nc.vector.tensor_tensor(before[:, j, :, :].rearrange("p g u -> p (g u)"), gate_ps[j][:, :],
                                            inputs[:, q, j * D:(j + 1) * D], ALU.add).then_inc(gate_read[j], 1)

                def update(j):
                    c = state[:, C, j * P:(j + 1) * P]
                    dve.wait_ge(gates_ready[j], count * 2 + 2)
                    nc.vector.tensor_tensor(kept[:, j, :], gates[:, j, 0, :], c, ALU.mult)
                    nc.vector.tensor_tensor(added[:, j, :], gates[:, j, 1, :], gates[:, j, 3, :],
                                            ALU.mult).then_inc(product_ready, 1)
                    dve.wait_ge(product_ready, count * KT + (j + 1))
                    nc.vector.tensor_tensor(c, kept[:, j, :], added[:, j, :], ALU.add).then_inc(c_ready[j], 1)

                def output(j):
                    if j == 0:
                        dve.wait_ge(result_ready, count + 1)
                    dve.wait_ge(squash_ready[j], count + 1)
                    nc.vector.tensor_tensor(state[:, H, j * P:(j + 1) * P], gates[:, j, 2, :], squashed[:, j, :],
                                            ALU.mult).then_inc(h_ready[j], 1)

                if k == CHECK_AT + 4:
                    dve.wait_ge(excess_ready, done + 1)
                    nc.vector.tensor_reduce(worst[:, :], excess[:, :, :], AX.XY, ALU.max).then_inc(worst_ready, 1)
                lower(2, count + 1)
                lower(3, count + 1)
                add(0)
                add(1)
                update(0)
                add(2)
                output(0)
                update(1)
                lower(0, count + sweep + 2)
                output(1)
                update(2)
                add(3)
                output(2)
                if not last:
                    lower(1, count + 2)
                update(3)
                output(3)

            dve.wait_ge(t.state_loaded, 16 * GATES * KT)
            for k in range(KT):
                nc.vector.tensor_copy(weights_high[:, k, :, :, :], t.state_weights[:, k, :, :, :]
                                      ).then_inc(weights_split, 1)
            for k in range(KT):
                dve.wait_ge(weights_split, k + 1)
                nc.vector.tensor_tensor(weights_low[:, k, :, :, :], t.state_weights[:, k, :, :, :],
                                        weights_high[:, k, :, :, :].bitcast(FP32), ALU.subtract
                                        ).then_inc(weights_split, 1)
            dve.wait_ge(history_ready, 2)

            def prologue(count):
                dve.wait_ge(turned[1], count + 1)
                nc.vector.tensor_copy(h_high[:, 1, :], turn_ps[1][:, :]).then_inc(high_ready[1], 1)
                lower(1, count + 1)

            sweeps(dve, begin, step, prologue)

        @block_.scalar
        def _(act):
            def heighten(j, value):
                act.wait_ge(turned[j], value)
                nc.scalar.activation(h_high[:, j, :], turn_ps[j][:, :], ACT.Copy).then_inc(high_ready[j], 1)
            
            def begin(sweep, steps):
                heighten(0, steps + sweep + 1)

            def step(sweep, done, b, pair, k, q):
                count = done * BLOCK + k
                last = k == BLOCK - 1

                def activate(j):
                    act.wait_ge(gate_read[j], count + 2)
                    nc.scalar.activation(gates[:, j, 0:3, :], before[:, j, 0:3, :], ACT.Sigmoid
                                         ).then_inc(gates_ready[j], 1)
                    nc.scalar.activation(gates[:, j, 3, :], before[:, j, 3, :], ACT.Tanh).then_inc(gates_ready[j], 1)

                def squash(j):
                    act.wait_ge(c_ready[j], count + 1)
                    nc.scalar.activation(squashed[:, j, :], state[:, C, j * P:(j + 1) * P], ACT.Tanh
                                         ).then_inc(squash_ready[j], 1)

                heighten(2, count + 1)
                heighten(3, count + 1)
                activate(0)
                activate(1)
                squash(0)
                activate(2)
                heighten(0, count + sweep + 2)
                squash(1)
                squash(2)
                if not last:
                    heighten(1, count + 2)
                activate(3)
                squash(3)
                if k == CHECK_AT:
                    act.wait_ge(h_ready[KT - 1], count + sweep + 3)
                    act.wait_ge(check, done * 5 + 1)
                    nc.scalar.activation(snap[:, :, :], state[:, :, :], ACT.Copy).then_inc(snapped, 1)

            sweeps(act, begin, step)

        @block_.tensor
        def _(pe):
            def turn(j, h_count):
                pe.wait_ge(h_ready[j], h_count)
                nc.tensor.transpose(turn_ps[j][:, :], state[:, H, j * P:(j + 1) * P], t.ident[:, :]
                                    ).then_inc(turned[j], 1)

            def begin(sweep, steps):
                pe.wait_ge(h_ready[KT - 1], steps + sweep + 1)
                nc.tensor.matmul(gate_ps[0][:, :], shift[:, :], state[:, C, :], start=True, stop=True
                                 ).then_inc(moved, 1)
                nc.tensor.matmul(gate_ps[1][:, :], shift[:, :], state[:, H, :], start=True, stop=True
                                 ).then_inc(moved, 1)
                turn(0, steps + sweep + 2)
                pe.wait_ge(c_moved, sweep + 1)
                hold(pe, h_ready[KT - 1], steps + sweep + 2, passed)

            def step(sweep, done, b, pair, k, q):
                count = done * BLOCK + k

                def high(j, kt):
                    if kt == 0:
                        pe.wait_ge(gate_read[j], count + 1)
                    for part, weights in enumerate((weights_high, weights_low)):
                        nc.tensor.matmul(gate_ps[j][:, :], h_high[:, kt, :],
                                         weights[:, kt, j, :, :].rearrange("p g u -> p (g u)"),
                                         start=(kt == 0 and part == 0), stop=False)

                def low(j, kt):
                    return nc.tensor.matmul(gate_ps[j][:, :], h_low[:, kt, :],
                                            weights_high[:, kt, j, :, :].rearrange("p g u -> p (g u)"),
                                            start=False, stop=(kt == KT - 1))

                pe.wait_ge(high_ready[0], count + sweep + 1)
                high(0, 0)
                turn(1, count + sweep + 2)
                high(1, 0)
                high(2, 0)
                pe.wait_ge(low_ready[0], count + sweep + 1)
                for j in range(3):
                    low(j, 0)
                pe.wait_ge(high_ready[1], count + 1)
                high(0, 1)
                turn(2, count + sweep + 2)
                high(1, 1)
                high(2, 1)
                pe.wait_ge(low_ready[1], count + 1)
                for j in range(3):
                    low(j, 1)
                pe.wait_ge(high_ready[2], count + 1)
                high(0, 2)
                turn(3, count + sweep + 2)
                high(3, 0)
                low(3, 0)
                pe.wait_ge(low_ready[2], count + 1)
                low(0, 2)
                pe.wait_ge(high_ready[3], count + 1)
                high(0, 3)
                pe.wait_ge(low_ready[3], count + 1)
                low(0, 3).then_inc(gate_done[0], 1)
                for j in (1, 2):
                    high(j, 2)
                    low(j, 2)
                    high(j, 3)
                    low(j, 3).then_inc(gate_done[j], 1)
                for kt in (1, 2):
                    high(3, kt)
                    low(3, kt)
                turn(0, count + sweep + 3)
                high(3, 3)
                low(3, 3).then_inc(gate_done[3], 1)

            pe.wait_ge(shift_ready, 2)
            pe.wait_ge(weights_split, 2 * KT)
            sweeps(pe, begin, step)


class Tables:
    pass


def gnn_lstm(nc, x, src, dst, W, b, gamma, beta, w_gates, b_gates, out):
    table = nc.dram_tensor("table", [ROWS, D], FP32, kind="Internal").ap()
    residual = nc.dram_tensor("residual", [ROWS, D], FP32, kind="Internal").ap()
    gate_in = nc.dram_tensor("gate_in", [ROWS, GATES * D], FP32, kind="Internal").ap()
    w_in = [w[0:D, :] for w in w_gates]
    w_state = [w[D:2 * D, :] for w in w_gates]
    ctx = ExitStack()
    with ctx:
        def sb(name, shape, dt):
            return ctx.enter_context(nc.sbuf_tensor(name, shape, dt))

        t = Tables()
        t.ident = sb("ident", [P, P], FP32)
        t.iota = sb("iota", [P, P], FP32)
        t.eps = sb("eps", [P, 1], FP32)
        with ExitStack() as graph:
            def gsb(name, shape, dt):
                return graph.enter_context(nc.sbuf_tensor(name, shape, dt))

            t.dst_f = gsb("dst_f", [P, EDGE_TILES], FP32)
            t.src_i = gsb("src_i", [P, EDGE_TILES], I32)
            t.node_base = gsb("node_base", [P, TILES], FP32)
            t.mask = gsb("mask", [P, TILES - FULL_TILES], FP32)
            t.publish_scale = gsb("publish_scale", [P, LAYERS, TILES], FP32)
            t.first_edge_tile = gsb("first_edge_tile", [1, TILES], I32)
            t.more_edge_tiles = gsb("more_edge_tiles", [1, TILES], I32)
            graph_tables(nc, dst, src, t)
            t.rows = gsb("rows", [P, TILES, D], FP32)
            input_norm(nc, x, table, t)
            graph_layers(nc, table, W, b, gamma, beta, t)
        t.state_weights = sb("state_weights", [P, KT, KT, GATES, P], FP32)
        t.state_loaded = ctx.enter_context(nc.semaphore("state_weights_loaded"))
        gate_inputs(nc, x, table, residual, gate_in, w_in, b_gates, w_state, t)
        recurrence(nc, residual, gate_in, out, t)


def kernel(x, src, dst, L0_gnn_W, L0_gnn_b, L0_gnn_gamma, L0_gnn_beta, L0_ffn_W_f, L0_ffn_b_f, L0_ffn_W_i,
           L0_ffn_b_i, L0_ffn_W_c, L0_ffn_b_c, L0_ffn_W_o, L0_ffn_b_o):
    import numpy as _np
    import concourse.bacc as _bacc
    from concourse import mybir as _mybir
    from concourse.bass_utils import run_bass_kernel_spmd as _run

    nc = _bacc.Bacc("TRN2", target_bir_lowering=False, num_devices=1)
    arrays = {
        "x": x, "src": src, "dst": dst, "gnn_w": L0_gnn_W, "gnn_b": L0_gnn_b, "gnn_gamma": L0_gnn_gamma,
        "gnn_beta": L0_gnn_beta, "w_f": L0_ffn_W_f, "w_i": L0_ffn_W_i, "w_o": L0_ffn_W_o, "w_c": L0_ffn_W_c,
        "b_f": L0_ffn_b_f, "b_i": L0_ffn_b_i, "b_o": L0_ffn_b_o, "b_c": L0_ffn_b_c,
    }
    arrays = {name: _np.ascontiguousarray(a) for name, a in arrays.items()}
    d = {name: nc.dram_tensor(f"{name}_in", a.shape, _mybir.dt.from_np(a.dtype), kind="ExternalInput").ap()
         for name, a in arrays.items()}
    out = nc.dram_tensor("out", [NODES, D], FP32, kind="ExternalOutput").ap()
    gnn_lstm(nc, d["x"], d["src"], d["dst"], d["gnn_w"], d["gnn_b"], d["gnn_gamma"], d["gnn_beta"],
             [d["w_f"], d["w_i"], d["w_o"], d["w_c"]], [d["b_f"], d["b_i"], d["b_o"], d["b_c"]], out)
    r = _run(nc, [{f"{name}_in": a for name, a in arrays.items()}], core_ids=[0])
    return r.results[0]["out"]
```
